# Optimizing a Trainium2 kernel written in Bass

```python
import numpy as np
import jax
import jax.numpy as jnp

def _softmax(x, axis=-1):
    return jax.nn.softmax(x, axis=axis)

def _gelu(x):
    return jax.nn.gelu(x, approximate=True)

def _silu(x):
    return jax.nn.silu(x)

def _sigmoid(x):
    return jax.nn.sigmoid(x)

def _layernorm(x, axis=-1, eps=1e-05):
    m = jnp.mean(x, axis=axis, keepdims=True)
    v = jnp.var(x, axis=axis, keepdims=True)
    return (x - m) / jnp.sqrt(v + eps)

def _scatter_add(tgt, idx, src, axis=0):
    return tgt.at[idx].add(src)

def _segment_sum(src, seg, n):
    return jax.ops.segment_sum(src, seg, n)
kernel_name = 'mk_decoder_preln_d1_seqx_r8_d394b6'

def setup_inputs(seed: int=0):
    np.random.seed(seed)
    _w = jnp.asarray

    def _rec_inputs():
        import jax
        import jax.numpy as jnp
        _rk = jax.random.key(seed)
        x = -0.0002928 + 1 * jax.random.normal(jax.random.fold_in(_rk, 1), (4, 512, 128), jnp.float32)
        _lenS = 512 - jax.random.randint(jax.random.fold_in(_rk, 7), (4,), 0, max(1, 512 // 4) + 1, jnp.int32)
        _lenS2 = 154 - jax.random.randint(jax.random.fold_in(_rk, 8), (4,), 0, max(1, 154 // 4) + 1, jnp.int32)
        _ctx_1024P = jax.random.normal(jax.random.fold_in(_rk, 11), (4, 16, 128), jnp.float32)
        _ctx_1024c = jax.random.dirichlet(jax.random.fold_in(_rk, 511), 0.3 * jnp.ones((16,), jnp.float32), (4, 154))
        _ctx_1024t = jnp.einsum('bsk,bkd->bsd', _ctx_1024c, _ctx_1024P)
        _ctx_1024t = _ctx_1024t * jax.lax.rsqrt(jnp.mean(jnp.square(_ctx_1024t)) + 1e-12) * 0.953939
        ctx_1024 = -1.39393e-06 + 0.999914 * (_ctx_1024t + 0.3 * jax.random.normal(jax.random.fold_in(_rk, 611), (4, 154, 128), jnp.float32))
        return (x, ctx_1024)
    x, ctx_1024 = _rec_inputs()

    def _L0_attn_setup():
        import jax, jax.numpy as jnp
        import numpy as np
        key = jax.random.key(seed)
        k1, = jax.random.split(key, 1)
        B, S, E = (4, 512, 128)
        x = jax.random.normal(k1, (B, S, E), dtype=jnp.float32)
        gamma = jnp.asarray(1.0, dtype=jnp.float32)
        return {'x': x, 'gamma': gamma}
    _L0_attn_all = _L0_attn_setup()
    _L0_attn_in = {k: v for k, v in _L0_attn_all.items() if k in ('gamma',)}
    del _L0_attn_all

    def _L0_xattn_setup():
        import math
        import jax, jax.numpy as jnp
        import numpy as np
        D_MODEL = 128
        N_HEADS = 16
        D_K = D_MODEL // N_HEADS

        def _alibi_slopes(n_heads):
            power = 2 ** math.ceil(math.log2(n_heads))
            slopes = np.array([2.0 ** (-8 + i) for i in range(power)], dtype=np.float32)
            if n_heads != power:
                ratio = power // n_heads
                slopes = slopes[np.arange(0, power, ratio)][:n_heads]
            return jnp.asarray(slopes)
        key = jax.random.key(seed)
        ks = jax.random.split(key, 11)
        B, S, D = (2, 256, D_MODEL)
        w = 0.02
        return {'query': jax.random.normal(ks[0], (B, S, D), jnp.float32), 'key': jax.random.normal(ks[1], (B, S, D), jnp.float32), 'value': jax.random.normal(ks[2], (B, S, D), jnp.float32), 'Wq': jax.random.normal(ks[3], (D, D), jnp.float32) * w, 'bq': jax.random.normal(ks[4], (D,), jnp.float32) * w, 'Wk': jax.random.normal(ks[5], (D, D), jnp.float32) * w, 'bk': jax.random.normal(ks[6], (D,), jnp.float32) * w, 'Wv': jax.random.normal(ks[7], (D, D), jnp.float32) * w, 'bv': jax.random.normal(ks[8], (D,), jnp.float32) * w, 'Wo': jax.random.normal(ks[9], (D, D), jnp.float32) * w, 'bo': jax.random.normal(ks[10], (D,), jnp.float32) * w}
    _L0_xattn_all = _L0_xattn_setup()
    _L0_xattn_in = {k: v for k, v in _L0_xattn_all.items() if k in ('Wq', 'bq', 'Wk', 'bk', 'Wv', 'bv', 'Wo', 'bo')}
    del _L0_xattn_all

    def _L0_ffn_setup():
        import jax, jax.numpy as jnp
        import numpy as np
        TOP_K = 2
        key = jax.random.key(seed)
        ks = jax.random.split(key, 5)
        B, S, H, E = (2, 128, 128, 8)
        return {'hidden_states': jax.random.normal(ks[0], (B, S, H), dtype=jnp.float32), 'router_w': jax.random.normal(ks[1], (E, H), dtype=jnp.float32) * 0.02, 'router_b': jax.random.normal(ks[2], (E,), dtype=jnp.float32) * 0.02, 'expert_w': jax.random.normal(ks[3], (E, H, H), dtype=jnp.float32) * 0.02, 'expert_b': jax.random.normal(ks[4], (E, H), dtype=jnp.float32) * 0.02}
    _L0_ffn_all = _L0_ffn_setup()
    _L0_ffn_in = {k: v for k, v in _L0_ffn_all.items() if k in ('router_w', 'router_b', 'expert_w', 'expert_b')}
    del _L0_ffn_all
    return {'x': x, 'ctx_1024': ctx_1024, 'L0_attn_gamma': _L0_attn_in['gamma'], 'L0_xattn_Wq': _L0_xattn_in['Wq'], 'L0_xattn_bq': _L0_xattn_in['bq'], 'L0_xattn_Wk': _L0_xattn_in['Wk'], 'L0_xattn_bk': _L0_xattn_in['bk'], 'L0_xattn_Wv': _L0_xattn_in['Wv'], 'L0_xattn_bv': _L0_xattn_in['bv'], 'L0_xattn_Wo': _L0_xattn_in['Wo'], 'L0_xattn_bo': _L0_xattn_in['bo'], 'L0_ffn_router_w': _L0_ffn_in['router_w'], 'L0_ffn_router_b': _L0_ffn_in['router_b'], 'L0_ffn_expert_w': _L0_ffn_in['expert_w'], 'L0_ffn_expert_b': _L0_ffn_in['expert_b']}

def reference(x, ctx_1024, L0_attn_gamma, L0_xattn_Wq, L0_xattn_bq, L0_xattn_Wk, L0_xattn_bk, L0_xattn_Wv, L0_xattn_bv, L0_xattn_Wo, L0_xattn_bo, L0_ffn_router_w, L0_ffn_router_b, L0_ffn_expert_w, L0_ffn_expert_b):
    import jax
    import jax.numpy as jnp

    def _L0_attn_ref(x, gamma):
        import jax, jax.numpy as jnp
        import numpy as np
        sq = jnp.sum(x * x, axis=-1)
        xy = jnp.einsum('bie,bje->bij', x, x)
        dist_sq = sq[:, :, None] + sq[:, None, :] - 2.0 * xy
        dist_sq = jnp.maximum(dist_sq, 0.0)
        attn = jax.nn.softmax(-gamma * dist_sq, axis=-1)
        return jnp.einsum('bij,bje->bie', attn, x)

    def _L0_xattn_ref(query, key, value, Wq, bq, Wk, bk, Wv, bv, Wo, bo):
        import math
        import jax, jax.numpy as jnp
        import numpy as np
        D_MODEL = 128
        N_HEADS = 16
        D_K = D_MODEL // N_HEADS

        def _alibi_slopes(n_heads):
            power = 2 ** math.ceil(math.log2(n_heads))
            slopes = np.array([2.0 ** (-8 + i) for i in range(power)], dtype=np.float32)
            if n_heads != power:
                ratio = power // n_heads
                slopes = slopes[np.arange(0, power, ratio)][:n_heads]
            return jnp.asarray(slopes)
        B, Sq, D = query.shape
        Sk = key.shape[1]
        H, dk = (N_HEADS, D_K)
        q = (query @ Wq.T + bq).reshape(B, Sq, H, dk).transpose(0, 2, 1, 3)
        k = (key @ Wk.T + bk).reshape(B, Sk, H, dk).transpose(0, 2, 1, 3)
        v = (value @ Wv.T + bv).reshape(B, Sk, H, dk).transpose(0, 2, 1, 3)
        scores = jnp.einsum('bhqd,bhkd->bhqk', q, k) / jnp.sqrt(jnp.float32(dk))
        dist = (jnp.arange(Sq)[:, None] - jnp.arange(Sk)[None, :]).astype(scores.dtype)
        slopes = _alibi_slopes(H)
        scores = scores + slopes[None, :, None, None] * dist[None, None, :, :]
        attn = jax.nn.softmax(scores, axis=-1)
        out = jnp.einsum('bhqk,bhkd->bhqd', attn, v)
        out = out.transpose(0, 2, 1, 3).reshape(B, Sq, D)
        return out @ Wo.T + bo

    def _L0_ffn_ref(hidden_states, router_w, router_b, expert_w, expert_b):
        import jax, jax.numpy as jnp
        import numpy as np
        TOP_K = 2
        logits = jnp.einsum('bsh,eh->bse', hidden_states, router_w) + router_b
        routing_weights = jax.nn.softmax(logits, axis=-1)
        _, top_k_indices = jax.lax.top_k(routing_weights, TOP_K)
        E = router_w.shape[0]
        mask = jax.nn.one_hot(top_k_indices, E, dtype=hidden_states.dtype).sum(axis=-2)
        out = jnp.einsum('bse,ehd,bsd->bsh', mask, expert_w, hidden_states)
        out = out + jnp.einsum('bse,eh->bsh', mask, expert_b)
        return out
    x = x + _L0_attn_ref(_layernorm(x, axis=-1), L0_attn_gamma)
    x = x + _L0_xattn_ref(_layernorm(x, axis=-1), ctx_1024, ctx_1024, L0_xattn_Wq, L0_xattn_bq, L0_xattn_Wk, L0_xattn_bk, L0_xattn_Wv, L0_xattn_bv, L0_xattn_Wo, L0_xattn_bo)
    x = x + _L0_ffn_ref(_layernorm(x, axis=-1), L0_ffn_router_w, L0_ffn_router_b, L0_ffn_expert_w, L0_ffn_expert_b)
    return x

_drawn_inputs = setup_inputs


def setup_inputs(seed=0):
    import zlib

    import numpy as np

    out = dict(_drawn_inputs(seed))
    spreads = {}
    factors = {'L0_xattn_Wq': 22.254,
     'L0_xattn_bq': 189.256,
     'L0_xattn_Wk': 21.854,
     'L0_xattn_bk': 200.0,
     'L0_xattn_bv': 8.0,
     'L0_ffn_expert_b': 4.103}
    for name, (base, spread) in spreads.items():
        noise = np.random.default_rng([zlib.crc32(name.encode()), seed]).standard_normal(out[name].shape)
        drawn = base * np.exp(spread * noise) if base else spread * noise
        out[name] = jnp.asarray(drawn.astype(out[name].dtype))
    for name, factor in factors.items():
        out[name] = (out[name] * factor).astype(out[name].dtype)
    return out
```

```python
import concourse.bass as bass
from concourse import mybir
from contextlib import ExitStack

B, S, D = 4, 512, 128
J = 154
H = 16
DK = D // H
E = 8
P = 128
T = S // P
JM = P
JT = J - JM
JP = JM + 32
G = 4
R = H // G
PAIRS = H // 2
HALF = P // 2
EPS = 1e-5
QSCALE = float(DK) ** -0.5

K_PART = (0, 1, 0, 1, 2, 0)
Q_PART = (0, 0, 1, 1, 0, 2)
AUG = DK * len(K_PART)
MAXROW = AUG + 3

ORDER = (
    ("Y", "scores", 0), ("X", "norm1", 0), ("Y", "scores", 1), ("Y", "values", 0), ("X", "dist", 0),
    ("W", "weights", 0), ("Y", "scores", 2), ("Y", "values", 1), ("X", "self", 0), ("Y", "scores", 3), ("Y", "values", 2),
    ("X", "gather", 0), ("Y", "values", 3), ("X", "query", 0), ("Y", "divide", 0), ("Y", "divide", 1),
    ("X", "maxima", 0), ("Y", "wo", 0), ("X", "maxima", 1), ("Y", "route", 0), ("X", "maxima", 2),
    ("Y", "mask", 0), ("X", "maxima", 3), ("X", "maxrow", 0), ("Y", "experts", 0), ("Y", "store", 0),
)


def walk(steps):
    for turn in range(B + 1):
        for stage, name, k in ORDER:
            b = turn - 1 if stage == "Y" else turn
            if 0 <= b < (1 if stage == "W" else B) and name in steps:
                steps[name](b, k)


def program(nc, x, ctx, gamma, Wq, bq, Wk, bk, Wv, bv, Wo, bo, rw, rb, ew, eb, q_aug, k_aug, out):
    F32, BF16 = mybir.dt.float32, mybir.dt.bfloat16
    ALU, ACT, AX = mybir.AluOpType, mybir.ActivationFunctionType, mybir.AxisListType
    with ExitStack() as stack:
        def sb(name, shape, dtype=F32):
            return stack.enter_context(nc.sbuf_tensor(name, shape, dtype))

        def sem(name):
            return stack.enter_context(nc.semaphore(name))

        bank = [stack.enter_context(nc.psum_tensor(f"bank{i}", [P, S], F32)) for i in range(8)]
        ST = bank[0:3]
        XR = bank[3:5]
        XM = bank[6]
        YV = bank[5]
        YM = bank[7]

        ident = sb("ident", [P, P])
        ident16 = sb("ident16", [P, P], BF16)
        ones = sb("ones", [P, P])
        ones16 = sb("ones16", [P, P], BF16)
        thirty_second = sb("thirty_second", [P, 1])
        minus_half = sb("minus_half", [P, T])
        pick = sb("pick", [P, E, P], BF16)
        earlier = sb("earlier", [P, E, E])
        gam = sb("gam", [P, 1])
        gam2 = sb("gam2", [P, 1])
        gneg = sb("gneg", [P, 1])
        sgn = sb("sgn", [P, 1])
        wraw = sb("wraw", [P, 4, P])
        wT = sb("wT", [P, 4, P])
        ewraw = sb("ewraw", [P, E, P])
        ewT = sb("ewT", [P, E, P])
        rwraw = sb("rwraw", [P, P])
        rwT = sb("rwT", [P, E])
        ebias = sb("ebias", [P, P])
        bqc = sb("bqc", [P, 1])
        bqs = sb("bqs", [P, 1])
        bkc = sb("bkc", [P, 1])
        bvb = sb("bvb", [P, P])
        bob = sb("bob", [P, P])
        rbb = sb("rbb", [P, E])
        ctx_m = sb("ctx_m", [P, B, D])
        ctx_t = sb("ctx_t", [32, B, D])
        ctxT = sb("ctxT", [P, B, JP])
        kf = sb("kf", [P, B, J])
        kr = sb("kr", [P, B, J])
        kpart = sb("kpart", [P, 3, B, J], BF16)
        kA = sb("kA", [P, PAIRS, 2, JP], BF16)
        kB = sb("kB", [P, PAIRS, 2, JP], BF16)
        vm = sb("vm", [P, B, H, 32])
        vt = sb("vt", [P, B, R, P])

        xs = sb("xs", [P, B, T, D])
        st1 = sb("st1", [P, T, 6])
        mv1 = sb("mv1", [P, T, 2])
        ve1 = sb("ve1", [P, T])
        rs1 = sb("rs1", [P, T])
        y1 = sb("y1", [P, T, D])
        y1T = sb("y1T", [P, S])
        y1Tg = sb("y1Tg", [P, S])
        nsq = sb("nsq", [P, T])
        nsr = sb("nsr", [P, T])
        nst = sb("nst", [P, T])
        snsq = sb("snsq", [P, T])
        sqp = sb("sqp", [P, T, P], BF16)
        sqT = sb("sqT", [P, S], BF16)
        rm = sb("rm", [P, T])
        rma = sb("rma", [P, T])
        rmb = sb("rmb", [P, T])
        diag = sb("diag", [P, T, P])
        ab = sb("ab", [P, S])
        w = sb("w", [P, T, S])
        oT = sb("oT", [P, S])
        dn = sb("dn", [P, S])
        rd1 = sb("rd1", [P, T])
        x1 = sb("x1", [P, T, D])
        st2 = sb("st2", [P, T, 6])
        mv2 = sb("mv2", [P, T, 2])
        ve2 = sb("ve2", [P, T])
        rs2 = sb("rs2", [P, T])
        y2 = sb("y2", [P, T, D])
        y2T = sb("y2T", [P, S])
        qf = sb("qf", [P, S])
        qr = sb("qr", [P, S])
        qpart = sb("qpart", [P, 3, S], BF16)
        nm = sb("nm", [P, T, H])
        nmr = sb("nmr", [P, T, H])
        mcat = sb("mcat", [P, T, 3, H], BF16)
        mT = sb("mT", [3 * H, S], BF16)
        qs = sb("qs", [P, 2, PAIRS, S], BF16)
        x1b = sb("x1b", [P, 2, T, D])
        PT_RING = 2 * (G + 1)
        pt = sb("pt", [P, PT_RING, S])
        pvs = sb("pvs", [P, 2, S])
        rd2 = sb("rd2", [P, T, PAIRS])
        ao = sb("ao", [P, T, P])
        aoT = sb("aoT", [P, S])
        x2 = sb("x2", [P, T, D])
        st3 = sb("st3", [P, T, 6])
        mv3 = sb("mv3", [P, T, 2])
        ve3 = sb("ve3", [P, T])
        rs3 = sb("rs3", [P, T])
        y3 = sb("y3", [P, T, D])
        y3T = sb("y3T", [P, S])
        lg = sb("lg", [P, T, E])
        cmp_eq = sb("cmp_eq", [P, T, E, E])
        cmp_gt = sb("cmp_gt", [P, T, E, E])
        rank = sb("rank", [P, T, E])
        maskp = sb("maskp", [P, T, P])
        maskT = sb("maskT", [P, S])
        maskT16 = sb("maskT16", [P, S], BF16)
        YM_RING = 3
        ym = sb("ym", [P, YM_RING, S])
        fT = sb("fT", [P, S])
        ob = sb("ob", [P, 2, T, D])

        k_scratch = nc.dram_tensor("k_scratch", [3, P, B, J], BF16, kind="Internal").ap()
        q_scratch = nc.dram_tensor("q_scratch", [3, P, S], BF16, kind="Internal").ap()
        m_scratch = nc.dram_tensor("m_scratch", [3, H, S], BF16, kind="Internal").ap()

        x_in = [sem(f"x_in{b}") for b in range(B)]
        gamma_in, weights_in, ctx_in = sem("gamma_in"), sem("weights_in"), sem("ctx_in")
        kaug_in, qaug_in = sem("kaug_in"), sem("qaug_in")
        k_out, q_out, m_out = sem("k_out"), sem("q_out"), sem("m_out")
        zeroed, consts = sem("zeroed"), sem("consts")
        gamma_ready, bqs_ready = sem("gamma_ready"), sem("bqs_ready")
        setup_ps, setup_sb = sem("setup_ps"), sem("setup_sb")
        k_ready, v_ready = sem("k_ready"), sem("v_ready")
        kA_in, kB_in, qs_in, m_in, stored = sem("kA_in"), sem("kB_in"), sem("qs_in"), sem("m_in"), sem("stored")
        stats = [sem(f"stats{i}") for i in range(3)]
        rstd = [sem(f"rstd{i}") for i in range(3)]
        normed = [sem(f"normed{i}") for i in range(3)]
        y1T_ps, sqT_ps, y1T_sb, sq_ready = sem("y1T_ps"), sem("sqT_ps"), sem("y1T_sb"), sem("sq_ready")
        dist_ps, rm_ready, w_relu, rowmax = sem("dist_ps"), sem("rm_ready"), sem("w_relu"), sem("rowmax")
        diag_ready, ab_ps, ab_sb = sem("diag_ready"), sem("ab_ps"), sem("ab_sb")
        w_sub, p_ready, self_ps, oT_sb, dn_sb = sem("w_sub"), sem("p_ready"), sem("self_ps"), sem("oT_sb"), sem("dn_sb")
        gather_ps, x1_ready, x1b_ready = sem("gather_ps"), sem("x1_ready"), sem("x1b_ready")
        y2T_ps, y2T_sb, q_ps, qf_ready = sem("y2T_ps"), sem("y2T_sb"), sem("q_ps"), sem("qf_ready")
        q_hi, q_rest, q_mid, q_lo = sem("q_hi"), sem("q_rest"), sem("q_mid"), sem("q_lo")
        a_ps, maxed, mcat_ready, mT_ps, mT_sb = sem("a_ps"), sem("maxed"), sem("mcat_ready"), sem("mT_ps"), sem("mT_sb")
        st_ps, exps, pv_ps, pvs_sb = sem("st_ps"), sem("exps"), sem("pv_ps"), sem("pvs_sb")
        nd_ps, ao_ready, ao_ps, aoT_sb, wo_ps, x2_ready = (
            sem("nd_ps"), sem("ao_ready"), sem("ao_ps"), sem("aoT_sb"), sem("wo_ps"), sem("x2_ready"))
        y3T_ps, y3T_sb, lg_ps, mask_ready, mask_ps, mask_sb = (
            sem("y3T_ps"), sem("y3T_sb"), sem("lg_ps"), sem("mask_ready"), sem("mask_ps"), sem("mask_sb"))
        mb_ps, masked, f_ps, fT_sb, fT_ps, out_ready = (
            sem("mb_ps"), sem("masked"), sem("f_ps"), sem("fT_sb"), sem("fT_ps"), sem("out_ready"))
        act_own, dve_own, pool_own = sem("act_own"), sem("dve_own"), sem("pool_own")

        def own(engine, semaphore):
            n = [0]

            def done(ins):
                n[0] += 1
                ins.then_inc(semaphore, 1)

            def settle():
                engine.wait_ge(semaphore, n[0])
            return done, settle

        def tile(t):
            return slice(t * P, (t + 1) * P)

        def col16(tensor):
            return tensor[:, :].bitcast(BF16)

        ITEMS = G + 1
        LAND = 16 * 2 * len(K_PART)
        block = stack.enter_context(nc.Block())

        @block.sync
        def _(sp):
            def load(dst, src, s):
                sp.dma_start(dst, src).then_inc(s, 16)

            load(xs[:, 0], x[0].rearrange("(t p) d -> p t d", p=P), x_in[0])
            load(gam[:, :], gamma.partition_broadcast(P), gamma_in)
            for i, m in enumerate((Wq, Wk, Wv)):
                load(wraw[:, i, :], m, weights_in)
            wo_view = Wo.rearrange("o (g f c) -> o f g c", g=G, f=2)
            for f in range(2):
                load(wraw[:, 3, f * HALF:(f + 1) * HALF].rearrange("o (g c) -> o g c", g=G), wo_view[:, f], weights_in)
            load(bqc[:, :], bq.rearrange("(p a) -> p a", a=1), weights_in)
            load(bkc[:, :], bk.rearrange("(p a) -> p a", a=1), weights_in)
            load(bvb[:, :], bv.partition_broadcast(P), weights_in)
            load(bob[:, :], bo.partition_broadcast(P), weights_in)
            load(rbb[:, :], rb.partition_broadcast(P), weights_in)
            load(ewraw[:, :, :], ew.rearrange("e h d -> h e d"), weights_in)
            load(ctx_m[:, :, :], ctx[:, 0:JM, :].rearrange("b j d -> j b d"), ctx_in)
            sp.wait_ge(zeroed, 3)
            load(ctx_t[0:JT, :, :], ctx[:, JM:J, :].rearrange("b j d -> j b d"), ctx_in)
            load(rwraw[0:E, :], rw, weights_in)
            load(ebias[0:E, :], eb, weights_in)
            load(kA[:, :, :, :], k_aug[0], kaug_in)
            load(kB[:, :, :, :], k_aug[1], kaug_in)
            for par in range(2):
                for s in range(2):
                    rows = slice(s * HALF + AUG, (s + 1) * HALF)
                    load(qs[rows, par, :, :], q_aug, qaug_in)
            for b in range(1, B):
                load(xs[:, b], x[b].rearrange("(t p) d -> p t d", p=P), x_in[b])

            def unstack(i, rows):
                return rows.rearrange("(a s c) n -> s c a n", s=2, c=DK)[i]

            def stack_keys(stacks, b, s_in):
                for r, part in enumerate(K_PART):
                    for s in range(2):
                        row = s * HALF + r * DK
                        load(stacks[row:row + DK, :, s, 0:J], unstack(s, k_scratch[part, :, b, :]), s_in)

            def norm1(b, _):
                if b >= 1:
                    sp.wait_ge(maxed, b * T * PAIRS)
                    stack_keys(kA, b, kA_in)

            def weights(b, _):
                sp.wait_ge(k_ready, 1)
                for part in range(3):
                    load(k_scratch[part], kpart[:, part], k_out)
                sp.wait_ge(k_out, 48)
                sp.wait_ge(kaug_in, 32)
                stack_keys(kA, b, kA_in)
                stack_keys(kB, b, kB_in)

            def query(b, _):
                for part, got in enumerate((q_hi, q_mid, q_lo)):
                    sp.wait_ge(got, b + 1)
                    load(q_scratch[part], qpart[:, part, :], q_out)
                if b == 0:
                    sp.wait_ge(qaug_in, 64)
                if b >= 2:
                    sp.wait_ge(st_ps, (b - 1) * R * ITEMS)
                sp.wait_ge(q_out, 48 * (b + 1))
                for r, part in enumerate(Q_PART):
                    for s in range(2):
                        row = s * HALF + r * DK
                        load(qs[row:row + DK, b % 2, :, :], unstack(s, q_scratch[part]), qs_in)
                if b >= 1:
                    sp.wait_ge(st_ps, b * R * ITEMS)
                    stack_keys(kB, b, kB_in)

            def maxrow(b, _):
                sp.wait_ge(mT_sb, b + 1)
                load(m_scratch.rearrange("i h n -> (i h) n"), mT[:, :], m_out)
                sp.wait_ge(m_out, 16 * (b + 1))
                for s in range(2):
                    row = s * HALF + MAXROW
                    load(qs[row:row + 3, b % 2, :, :], m_scratch.rearrange("i (a s) n -> s i a n", s=2)[s], m_in)

            def store(b, _):
                sp.wait_ge(out_ready, b + 1)
                load(out[b].rearrange("(t p) d -> p t d", p=P), ob[:, b % 2], stored)

            walk({"norm1": norm1, "weights": weights, "query": query, "maxrow": maxrow, "store": store})
            sp.wait_ge(stored, 16 * B)

        @block.gpsimd
        def _(pool):
            done, settle = own(pool, pool_own)
            g = nc.gpsimd
            done(g.memset(ident[:, :], 0.0))
            done(g.memset(ident16[:, :], 0.0))
            g.memset(ctx_t[:, :, :], 0.0).then_inc(zeroed, 1)
            g.memset(rwraw[:, :], 0.0).then_inc(zeroed, 1)
            g.memset(ebias[:, :], 0.0).then_inc(zeroed, 1)
            done(g.memset(minus_half[:, :], -0.5))
            settle()
            for m in (ident, ident16):
                g.affine_select(out=m[:, :], in_=m[:, :], compare_op=ALU.not_equal, fill=1.0, base=0,
                                pattern=[[-1, P]], channel_multiplier=1).then_inc(consts, 1)
            g.memset(sqp[:, :, :], 0.0).then_inc(consts, 1)
            g.memset(ones16[:, :], 1.0).then_inc(consts, 1)
            g.memset(ones[:, :], 1.0).then_inc(consts, 1)
            g.memset(thirty_second[:, :], 1.0 / 32).then_inc(consts, 1)
            pool.wait_ge(consts, 6)
            pool.wait_ge(gamma_in, 16)
            done(g.tensor_scalar(gam2[:, :], gam[:, :], 2.0, 1.0, ALU.mult, ALU.mult))
            done(g.tensor_scalar(gneg[:, :], gam[:, :], -float(D), 1.0, ALU.mult, ALU.mult))
            done(g.tensor_scalar(rma[:, 0:1], gam[:, :], 0.0, None, ALU.is_lt))
            settle()
            g.tensor_scalar(sgn[:, :], rma[:, 0:1], 2.0, -1.0, ALU.mult, ALU.add).then_inc(gamma_ready, 1)
            pool.wait_ge(gamma_ready, 1)

            def norm(i, b, mv, ve, rs):
                pool.wait_ge(stats[i], b + 1)
                done(g.tensor_scalar(ve[:, :], mv[:, :, 1], EPS, 1.0, ALU.add, ALU.mult))
                settle()
                g.tensor_tensor(rs[:, :], ve[:, :], minus_half[:, :], ALU.pow).then_inc(rstd[i], 1)

            def three(dst, value, rest, last, last_sem):
                done(g.tensor_copy(dst(0), value))
                settle()
                done(g.tensor_tensor(rest, value, dst(0), ALU.subtract))
                settle()
                done(g.tensor_copy(dst(1), rest))
                settle()
                done(g.tensor_tensor(last, rest, dst(1), ALU.subtract))
                settle()
                g.tensor_copy(dst(2), last).then_inc(last_sem, 1)

            def norm1(b, _):
                norm(0, b, mv1, ve1, rs1)
                pool.wait_ge(rstd[0], b + 1)
                done(g.tensor_tensor(nsr[:, :], rs1[:, :], rs1[:, :], ALU.mult))
                settle()
                done(g.tensor_tensor(nst[:, :], nsr[:, :], mv1[:, :, 1], ALU.mult))
                settle()
                done(g.tensor_scalar(nsq[:, :], nst[:, :], gneg[:, :], 1.0, ALU.mult, ALU.mult))
                settle()
                done(g.tensor_scalar(snsq[:, :], nsq[:, :], sgn[:, :], 1.0, ALU.mult, ALU.mult))
                three(lambda i: sqp[:, :, i], nsq[:, :], nsr[:, :], nst[:, :], sq_ready)

            def weights(b, _):
                pool.wait_ge(weights_in, 16 * 13)
                g.tensor_scalar(bqs[:, :], bqc[:, :], QSCALE, 1.0, ALU.mult, ALU.mult).then_inc(bqs_ready, 1)
                done(g.memset(pick[:, :, :], 0.0))
                done(g.memset(earlier[:, :, :], 1.0))
                done(g.memset(maskp[:, :, :], 0.0))
                settle()
                g.affine_select(out=pick[:, :, :], in_=pick[:, :, :], compare_op=ALU.not_equal, fill=1.0, base=0,
                                pattern=[[-1, E], [0, P]], channel_multiplier=1).then_inc(consts, 1)
                g.affine_select(out=earlier[:, :, :], in_=earlier[:, :, :], compare_op=ALU.is_gt, fill=0.0, base=0,
                                pattern=[[1, E], [-1, E]], channel_multiplier=0).then_inc(consts, 1)

            def self_(b, _):
                pool.wait_ge(rowmax, b + 1)
                for t in range(T):
                    last = g.tensor_scalar(diag[:, t, :], ident[:, :], rmb[:, t:t + 1], 1.0, ALU.mult, ALU.mult)
                last.then_inc(diag_ready, 1)
                pool.wait_ge(ab_sb, b + 1)
                pool.wait_ge(w_relu, T * (b + 1))
                for t in range(T):
                    g.tensor_tensor(w[:, t, :], w[:, t, :], ab[:, :], ALU.subtract).then_inc(w_sub, 1)

            def gather(b, _):
                norm(1, b, mv2, ve2, rs2)
                pool.wait_ge(x1_ready, b + 1)
                if b == 0:
                    pool.wait_ge(weights_in, 16 * 13)
                g.tensor_tensor(x1b[:, b % 2], x1[:, :, :], bob[:, :].unsqueeze(1).broadcast_to([P, T, D]),
                                ALU.add).then_inc(x1b_ready, 1)

            def query(b, _):
                pool.wait_ge(q_hi, b + 1)
                g.tensor_tensor(qr[:, :], qf[:, :], qpart[:, 0, :], ALU.subtract).then_inc(q_rest, 1)
                pool.wait_ge(q_mid, b + 1)
                g.tensor_tensor(qpart[:, 2, :], qr[:, :], qpart[:, 1, :], ALU.subtract).then_inc(q_lo, 1)

            def maxrow(b, _):
                pool.wait_ge(maxed, (b + 1) * T * PAIRS)
                three(lambda i: mcat[:, :, i, :], nm[:, :, :], nmr[:, :, :], nmr[:, :, :], mcat_ready)

            def wo(b, _):
                norm(2, b, mv3, ve3, rs3)

            walk({"norm1": norm1, "weights": weights, "self": self_, "gather": gather, "query": query,
                  "maxrow": maxrow, "wo": wo})

        @block.scalar
        def _(act):
            done, settle = own(act, act_own)
            copy = lambda dst, src: nc.scalar.activation(dst, src, ACT.Copy)

            def dist(b, _):
                if b == 0:
                    act.wait_ge(gamma_ready, 1)
                act.wait_ge(y1T_ps, b + 1)
                copy(y1T[:, :], XM[:, :]).then_inc(y1T_sb, 1)
                nc.scalar.activation(y1Tg[:, :], XM[:, :], ACT.Copy, scale=gam2[:, :]).then_inc(y1T_sb, 1)
                act.wait_ge(sqT_ps, b + 1)
                copy(sqT[:, :], col16(XR[1])[:, 0:S]).then_inc(y1T_sb, 1)
                for t in range(T):
                    act.wait_ge(rm_ready, T * b + t + 1)
                    nc.scalar.activation(w[:, t, :], XR[t % 2][:, :], ACT.Relu, bias=snsq[:, t:t + 1],
                                         scale=sgn[:, :]).then_inc(w_relu, 1)

            def self_(b, _):
                act.wait_ge(ab_ps, b + 1)
                copy(ab[:, :], XM[:, :]).then_inc(ab_sb, 1)
                for t in range(T):
                    act.wait_ge(w_sub, T * b + t + 1)
                    nc.scalar.activation(w[:, t, :], w[:, t, :], ACT.Exp, scale=sgn[:, :]).then_inc(p_ready, 1)
                act.wait_ge(self_ps, b + 1)
                copy(oT[:, :], XR[0][:, :]).then_inc(oT_sb, 1)

            def weights(b, _):
                act.wait_ge(setup_ps, 1)
                copy(wT[:, :, :], ST[0][:, :].rearrange("p (i n) -> p i n", i=4)).then_inc(setup_sb, 1)
                for i in range(2):
                    copy(ewT[:, 4 * i:4 * i + 4, :], ST[1 + i][:, :].rearrange("p (i n) -> p i n", i=4)).then_inc(setup_sb, 1)
                copy(rwT[:, :], YV[:, 0:E]).then_inc(setup_sb, 1)
                copy(ctxT[:, :, 0:JM], YM[:, :].rearrange("p (b j) -> p b j", b=B)).then_inc(setup_sb, 1)
                act.wait_ge(setup_ps, 2)
                copy(ctxT[:, :, JM:JP], ST[0][:, 0:32 * B].rearrange("p (b j) -> p b j", b=B)).then_inc(setup_sb, 1)
                act.wait_ge(setup_ps, 3)
                act.wait_ge(weights_in, 16 * 13)
                for i in range(2):
                    nc.scalar.activation(kf[:, 2 * i:2 * i + 2, :],
                                         ST[1 + i][:, 0:2 * J].rearrange("p (b j) -> p b j", b=2),
                                         ACT.Identity, bias=bkc[:, :]).then_inc(setup_sb, 1)

            def query(b, _):
                act.wait_ge(y2T_ps, b + 1)
                copy(y2T[:, :], XM[:, :]).then_inc(y2T_sb, 1)
                act.wait_ge(q_ps, b + 1)
                if b == 0:
                    act.wait_ge(bqs_ready, 1)
                nc.scalar.activation(qf[:, :], XR[0][:, :], ACT.Identity, bias=bqs[:, :],
                                     scale=QSCALE).then_inc(qf_ready, 1)
                act.wait_ge(qf_ready, b + 1)
                copy(qpart[:, 0, :], qf[:, :]).then_inc(q_hi, 1)

            def maxrow(b, _):
                act.wait_ge(mT_ps, b + 1)
                copy(mT[:, :], col16(XM)[0:3 * H, 0:S]).then_inc(mT_sb, 1)

            def scores(b, k):
                for i in range(ITEMS):
                    n = (b * R + k) * ITEMS + i
                    act.wait_ge(st_ps, n + 1)
                    if n >= PT_RING:
                        act.wait_ge(pv_ps, b * R + k - 1)
                    nc.scalar.activation(pt[:, n % PT_RING, :], ST[n % 3][:, :], ACT.Exp).then_inc(exps, 1)

            def values(b, k):
                if k % 2:
                    act.wait_ge(pv_ps, b * R + k + 1)
                    copy(pvs[:, k // 2, :], YV[:, :]).then_inc(pvs_sb, 1)

            def wo(b, _):
                act.wait_ge(ao_ps, b + 1)
                copy(aoT[:, :], YM[:, :]).then_inc(aoT_sb, 1)

            def route(b, _):
                act.wait_ge(y3T_ps, b + 1)
                copy(y3T[:, :], YM[:, :]).then_inc(y3T_sb, 1)

            def mask(b, _):
                act.wait_ge(mask_ps, b + 1)
                copy(maskT[:, :], YM[:, :]).then_inc(mask_sb, 1)
                act.wait_ge(mask_sb, 2 * b + 1)
                copy(maskT16[:, :], maskT[:, :]).then_inc(mask_sb, 1)

            def store(b, _):
                act.wait_ge(f_ps, E * (b + 1))
                copy(fT[:, :], YV[:, :]).then_inc(fT_sb, 1)

            walk({"dist": dist, "self": self_, "weights": weights, "query": query, "maxrow": maxrow, "scores": scores,
                  "values": values, "wo": wo, "route": route, "mask": mask, "store": store})

        @block.vector
        def _(dve):
            done, settle = own(dve, dve_own)
            v = nc.vector

            def norm(i, b, src, st, mv, rs, y):
                for t in range(T):
                    done(v.bn_stats(st[:, t, :], src(t)))
                settle()
                for t in range(T):
                    last = v.bn_aggr(mv[:, t, :], st[:, t, :])
                last.then_inc(stats[i], 1)
                dve.wait_ge(stats[i], b + 1)
                dve.wait_ge(rstd[i], b + 1)
                for t in range(T):
                    last = v.tensor_scalar(y[:, t, :], src(t), mv[:, t, 0:1], rs[:, t:t + 1], ALU.subtract, ALU.mult)
                last.then_inc(normed[i], 1)

            def norm1(b, _):
                dve.wait_ge(x_in[b], 16)
                norm(0, b, lambda t: xs[:, b, t, :], st1, mv1, rs1, y1)

            def dist(b, _):
                for t in range(T):
                    dve.wait_ge(dist_ps, T * b + t + 1)
                    v.tensor_reduce(rm[:, t:t + 1], XR[t % 2][:, :], AX.X, ALU.max).then_inc(rm_ready, 1)
                dve.wait_ge(rm_ready, T * (b + 1))
                dve.wait_ge(sq_ready, b + 1)
                done(v.scalar_tensor_tensor(out=rma[:, :], in0=rm[:, :], scalar=sgn[:, :], in1=snsq[:, :],
                                            op0=ALU.mult, op1=ALU.add))
                settle()
                v.tensor_scalar(rmb[:, :], rma[:, :], 0.0, None, ALU.max).then_inc(rowmax, 1)

            def self_(b, _):
                dve.wait_ge(self_ps, b + 1)
                v.tensor_copy(dn[:, :], XR[1][:, :]).then_inc(dn_sb, 1)

            def gather(b, _):
                dve.wait_ge(gather_ps, b + 1)
                done(v.reciprocal(rd1[:, :], XR[0][:, 0:T]))
                settle()
                for t in range(T):
                    last = v.scalar_tensor_tensor(out=x1[:, t, :], in0=XM[:, tile(t)], scalar=rd1[:, t:t + 1],
                                                  in1=xs[:, b, t, :], op0=ALU.mult, op1=ALU.add)
                last.then_inc(x1_ready, 1)
                dve.wait_ge(x1_ready, b + 1)
                norm(1, b, lambda t: x1[:, t, :], st2, mv2, rs2, y2)

            def weights(b, _):
                done(v.memset(vm[:, :, :, :], 0.0))
                done(v.memset(vt[:, :, :, :], 0.0))
                settle()
                for s in range(2):
                    done(v.memset(vm[:, :, s::2, 16 * s + DK:16 * s + 2 * DK], 1.0))
                    for g in range(G):
                        c = 32 * g + 16 * s
                        done(v.memset(vt[32 * g:32 * g + JT, :, s::2, c + DK:c + 2 * DK], 1.0))
                dve.wait_ge(setup_ps, 3)
                dve.wait_ge(weights_in, 16 * 13)
                for b in range(B):
                    val = YM[:, tile(b)].rearrange("p (a s d) -> p s a d", s=2, d=DK)
                    bias = bvb[:, :].rearrange("p (a s d) -> p s a d", s=2, d=DK)
                    for s in range(2):
                        done(v.tensor_tensor(vm[:, b, s::2, 16 * s:16 * s + DK], val[:, s], bias[:, s], ALU.add))
                for g in range(G):
                    rows = slice(32 * g, 32 * g + JT)
                    val = YV[rows, 0:32 * B].rearrange("p (b a s d) -> p s b a d", b=B, s=2, d=DK)
                    bias = bvb[rows, 32 * g:32 * g + 32].rearrange("p (a s d) -> p s a d", s=2, d=DK)
                    for s in range(2):
                        c = 32 * g + 16 * s
                        done(v.tensor_tensor(vt[rows, :, s::2, c:c + DK], val[:, s],
                                             bias[:, s].unsqueeze(1).broadcast_to([JT, B, 2, DK]), ALU.add))
                settle()
                dve.wait_ge(setup_sb, 8)
                v.tensor_copy(kpart[:, 0], kf[:, :, :]).then_inc(v_ready, 1)
                dve.wait_ge(v_ready, 1)
                done(v.tensor_tensor(kr[:, :, :], kf[:, :, :], kpart[:, 0], ALU.subtract))
                settle()
                done(v.tensor_copy(kpart[:, 1], kr[:, :, :]))
                settle()
                v.tensor_tensor(kpart[:, 2], kr[:, :, :], kpart[:, 1], ALU.subtract).then_inc(k_ready, 1)

            def query(b, _):
                dve.wait_ge(q_rest, b + 1)
                v.tensor_copy(qpart[:, 1, :], qr[:, :]).then_inc(q_mid, 1)

            def maxima(b, t):
                for a in range(PAIRS):
                    dve.wait_ge(a_ps, (b * T + t) * PAIRS + a + 1)
                    v.tensor_reduce(nm[:, t, 2 * a:2 * a + 2], XR[a % 2][:, 0:2 * J].rearrange("p (s j) -> p s j", s=2),
                                    AX.X, ALU.max, negate=True).then_inc(maxed, 1)

            def divide(b, f):
                nd = YM[:, :].rearrange("p (t c x) -> p t c x", t=T, x=2 * DK)
                dve.wait_ge(nd_ps, 2 * b + f + 1)
                done(v.reciprocal(rd2[:, :, :], nd[:, :, :, DK]))
                settle()
                v.tensor_tensor(ao[:, :, f * HALF:(f + 1) * HALF].rearrange("p t (c d) -> p t c d", d=DK),
                                nd[:, :, :, 0:DK], rd2[:, :, :].unsqueeze(3).broadcast_to([P, T, PAIRS, DK]),
                                ALU.mult).then_inc(ao_ready, 1)

            def wo(b, _):
                dve.wait_ge(wo_ps, b + 1)
                dve.wait_ge(x1b_ready, b + 1)
                v.tensor_tensor(x2[:, :, :], YV[:, :].rearrange("p (t d) -> p t d", t=T), x1b[:, b % 2],
                                ALU.add).then_inc(x2_ready, 1)
                dve.wait_ge(x2_ready, b + 1)
                norm(2, b, lambda t: x2[:, t, :], st3, mv3, rs3, y3)

            def mask(b, _):
                dve.wait_ge(lg_ps, b + 1)
                if b == 0:
                    dve.wait_ge(consts, 8)
                done(v.tensor_tensor(lg[:, :, :], YV[:, 0:T * E].rearrange("p (t e) -> p t e", t=T),
                                     rbb[:, :].unsqueeze(1).broadcast_to([P, T, E]), ALU.add))
                settle()
                other = lg[:, :, :].unsqueeze(2).broadcast_to([P, T, E, E])
                mine = lg[:, :, :].unsqueeze(3).broadcast_to([P, T, E, E])
                done(v.tensor_tensor(cmp_eq[:, :, :, :], other, mine, ALU.is_equal))
                done(v.tensor_tensor(cmp_gt[:, :, :, :], other, mine, ALU.is_gt))
                settle()
                done(v.tensor_tensor(cmp_eq[:, :, :, :], cmp_eq[:, :, :, :],
                                     earlier[:, :, :].unsqueeze(1).broadcast_to([P, T, E, E]), ALU.mult))
                settle()
                done(v.tensor_tensor(cmp_gt[:, :, :, :], cmp_gt[:, :, :, :], cmp_eq[:, :, :, :], ALU.add))
                settle()
                done(v.tensor_reduce(rank[:, :, :], cmp_gt[:, :, :, :], AX.X, ALU.add))
                settle()
                v.tensor_scalar(maskp[:, :, 0:E], rank[:, :, :], 1.5, None, ALU.is_lt).then_inc(mask_ready, 1)

            def experts(b, _):
                for e in range(E):
                    n = E * b + e
                    dve.wait_ge(mb_ps, n + 1)
                    if n >= YM_RING:
                        dve.wait_ge(f_ps, n - YM_RING + 1)
                    v.tensor_tensor(ym[:, n % YM_RING, :], ST[e % 3][:, :], y3T[:, :], ALU.mult).then_inc(masked, 1)

            def store(b, _):
                dve.wait_ge(fT_ps, b + 1)
                if b >= 2:
                    dve.wait_ge(stored, 16 * (b - 1))
                v.tensor_tensor(ob[:, b % 2], YM[:, :].rearrange("p (t d) -> p t d", t=T), x2[:, :, :],
                                ALU.add).then_inc(out_ready, 1)

            walk({"norm1": norm1, "dist": dist, "self": self_, "gather": gather, "weights": weights, "query": query,
                  "maxima": maxima, "divide": divide, "wo": wo, "mask": mask, "experts": experts, "store": store})

        @block.tensor
        def _(pe):
            mm = nc.tensor.matmul
            pe.wait_ge(consts, 6)

            def turn(bank_, src, id_=ident):
                for t in range(T):
                    last = nc.tensor.transpose(bank_[:, tile(t)], src(t), id_[:, :])
                return last

            def weights(b, _):
                pe.wait_ge(weights_in, 16 * 13)
                pe.wait_ge(ctx_in, 32)
                turn(ST[0], lambda i: wraw[:, i, :])
                turn(ST[1], lambda i: ewraw[:, i, :])
                turn(ST[2], lambda i: ewraw[:, 4 + i, :])
                nc.tensor.transpose(YV[:, 0:P], rwraw[:, :], ident[:, :])
                turn(YM, lambda i: ctx_m[:, i, :]).then_inc(setup_ps, 1)
                pe.wait_ge(setup_sb, 5)
                for i in range(B):
                    last = nc.tensor.transpose(ST[0][:, 32 * i:32 * i + 32], ctx_t[:, i, :], ident[0:32, 0:32])
                last.then_inc(setup_ps, 1)
                pe.wait_ge(setup_sb, 6)
                for i in range(2):
                    mm(ST[1 + i][:, 0:2 * J], wT[:, 1, :], ctxT[:, 2 * i:2 * i + 2, 0:J], start=True, stop=True)
                for i in range(B):
                    mm(YM[:, tile(i)], ctxT[:, i, 0:JM], wT[:, 2, :], start=True, stop=True)
                for i in range(B):
                    for g in range(G):
                        last = mm(YV[32 * g:32 * g + 32, 32 * i:32 * i + 32], ctxT[:, i, JM:JP],
                                  wT[:, 2, 32 * g:32 * g + 32], start=True, stop=True)
                last.then_inc(setup_ps, 1)

            def dist(b, _):
                pe.wait_ge(normed[0], b + 1)
                if b >= 1:
                    pe.wait_ge(mT_sb, b)
                    pe.wait_ge(maxed, b * T * PAIRS)
                turn(XM, lambda t: y1[:, t, :]).then_inc(y1T_ps, 1)
                pe.wait_ge(sq_ready, b + 1)
                turn(col16(XR[1]), lambda t: sqp[:, t, :], ident16).then_inc(sqT_ps, 1)
                pe.wait_ge(y1T_sb, 3 * (b + 1))
                for t in range(T):
                    if t >= 2:
                        pe.wait_ge(w_relu, T * b + t - 1)
                    mm(XR[t % 2][:, :], y1T[:, tile(t)], y1Tg[:, :], start=True, stop=False)
                    mm(XR[t % 2][:, :], ones16[:, :], sqT[:, :], start=False, stop=True).then_inc(dist_ps, 1)

            def self_(b, _):
                pe.wait_ge(diag_ready, b + 1)
                mm(XM[:, :], ones[:, :], diag[:, :, :], start=True, stop=True).then_inc(ab_ps, 1)
                pe.wait_ge(w_relu, T * (b + 1))
                for t in range(T):
                    pe.wait_ge(p_ready, T * b + t + 1)
                    mm(XR[0][:, :], y1[:, t, :], w[:, t, :], start=(t == 0), stop=(t == T - 1))
                for t in range(T):
                    last = mm(XR[1][32 * t:32 * t + 32, :], ones[:, 0:32], w[:, t, :], start=True, stop=True)
                last.then_inc(self_ps, 1)

            def gather(b, _):
                pe.wait_ge(oT_sb, b + 1)
                pe.wait_ge(dn_sb, b + 1)
                turn(XM, lambda t: oT[:, tile(t)])
                for t in range(T):
                    last = mm(XR[0][:, t:t + 1], dn[:, tile(t)], thirty_second[:, :], start=True, stop=True)
                last.then_inc(gather_ps, 1)

            def query(b, _):
                pe.wait_ge(normed[1], b + 1)
                turn(XM, lambda t: y2[:, t, :]).then_inc(y2T_ps, 1)
                pe.wait_ge(y2T_sb, b + 1)
                if b == 0:
                    pe.wait_ge(setup_sb, 8)
                mm(XR[0][:, :], wT[:, 0, :], y2T[:, :], start=True, stop=True).then_inc(q_ps, 1)

            def maxima(b, t):
                if t == 0:
                    pe.wait_ge(kA_in, LAND * (b + 1))
                    pe.wait_ge(qs_in, LAND * (b + 1))
                    pe.wait_ge(qf_ready, b + 1)
                for a in range(PAIRS):
                    n = (b * T + t) * PAIRS + a
                    if t or a >= 2:
                        pe.wait_ge(maxed, n - 1)
                    mm(XR[a % 2][:, 0:2 * J], qs[:, b % 2, a, tile(t)], kA[:, a, :, 0:J],
                       start=True, stop=True).then_inc(a_ps, 1)

            def maxrow(b, _):
                pe.wait_ge(mcat_ready, b + 1)
                turn(col16(XM)[0:3 * H], lambda t: mcat[:, t, :, :].rearrange("p i h -> p (i h)"),
                     ident16).then_inc(mT_ps, 1)

            def scores(b, k):
                if k == 0:
                    pe.wait_ge(kB_in, LAND * (b + 1))
                    pe.wait_ge(m_in, 32 * (b + 1))
                    if b >= 1:
                        pe.wait_ge(masked, E * b)
                for i in range(ITEMS):
                    n = (b * R + k) * ITEMS + i
                    if n >= 3:
                        pe.wait_ge(exps, n - 2)
                    if i < G:
                        h = R * i + k
                        last = mm(ST[n % 3][:, :], kB[:, h // 2, h % 2, 0:JM], qs[:, b % 2, h // 2, :],
                                  start=True, stop=True)
                    else:
                        for g in range(G):
                            h = R * g + k
                            last = mm(ST[n % 3][32 * g:32 * g + 32, :], kB[:, h // 2, h % 2, JM:JP],
                                      qs[:, b % 2, h // 2, :], start=True, stop=True)
                    last.then_inc(st_ps, 1)

            def values(b, k):
                n = (b * R + k) * ITEMS
                if k == 0 and b == 0:
                    pe.wait_ge(v_ready, 1)
                if k == 0 and b >= 1:
                    pe.wait_ge(fT_sb, b)
                if k == 2:
                    pe.wait_ge(pvs_sb, 2 * b + 1)
                pe.wait_ge(exps, n + ITEMS)
                for g in range(G):
                    mm(YV[32 * g:32 * g + 32, :], vm[:, b, R * g + k, :], pt[:, (n + g) % PT_RING, :],
                       start=(k % 2 == 0), stop=False, skip_group_check=True)
                mm(YV[:, :], vt[:, b, k, :], pt[:, (n + G) % PT_RING, :], start=False, stop=(k % 2 == 1),
                   skip_group_check=True).then_inc(pv_ps, 1)

            def divide(b, f):
                pe.wait_ge(pvs_sb, 2 * b + f + 1)
                if f == 0 and b >= 1:
                    pe.wait_ge(out_ready, b)
                if f == 1:
                    pe.wait_ge(ao_ready, 2 * b + 1)
                turn(YM, lambda t: pvs[:, f, tile(t)]).then_inc(nd_ps, 1)

            def wo(b, _):
                pe.wait_ge(ao_ready, 2 * b + 2)
                turn(YM, lambda t: ao[:, t, :]).then_inc(ao_ps, 1)
                pe.wait_ge(aoT_sb, b + 1)
                for t in range(T):
                    last = mm(YV[:, tile(t)], aoT[:, tile(t)], wT[:, 3, :], start=True, stop=True)
                last.then_inc(wo_ps, 1)

            def route(b, _):
                pe.wait_ge(normed[2], b + 1)
                turn(YM, lambda t: y3[:, t, :]).then_inc(y3T_ps, 1)
                pe.wait_ge(y3T_sb, b + 1)
                for t in range(T):
                    last = mm(YV[:, t * E:(t + 1) * E], y3T[:, tile(t)], rwT[:, :], start=True, stop=True)
                last.then_inc(lg_ps, 1)

            def mask(b, _):
                pe.wait_ge(mask_ready, b + 1)
                turn(YM, lambda t: maskp[:, t, :]).then_inc(mask_ps, 1)

            def experts(b, _):
                def spread(e):
                    if e >= 3:
                        pe.wait_ge(masked, E * b + e - 2)
                    mm(ST[e % 3][:, :], pick[:, e, :], maskT16[:, :], start=True, stop=True).then_inc(mb_ps, 1)

                pe.wait_ge(mask_sb, 2 * (b + 1))
                mm(YV[:, :], ebias[:, :], maskT[:, :], start=True, stop=False)
                pe.wait_ge(exps, (b + 1) * R * ITEMS)
                spread(0)
                spread(1)
                for e in range(E):
                    if e + 2 < E:
                        spread(e + 2)
                    pe.wait_ge(masked, E * b + e + 1)
                    mm(YV[:, :], ewT[:, e, :], ym[:, (E * b + e) % YM_RING, :], start=False,
                       stop=(e == E - 1)).then_inc(f_ps, 1)

            def store(b, _):
                pe.wait_ge(fT_sb, b + 1)
                turn(YM, lambda t: fT[:, tile(t)]).then_inc(fT_ps, 1)

            walk({"dist": dist, "self": self_, "gather": gather, "weights": weights, "query": query, "maxima": maxima,
                  "maxrow": maxrow, "scores": scores, "values": values, "divide": divide, "wo": wo, "route": route,
                  "mask": mask, "experts": experts, "store": store})


_INS = ['x', 'ctx_1024', 'L0_attn_gamma', 'L0_xattn_Wq', 'L0_xattn_bq', 'L0_xattn_Wk', 'L0_xattn_bk', 'L0_xattn_Wv',
        'L0_xattn_bv', 'L0_xattn_Wo', 'L0_xattn_bo', 'L0_ffn_router_w', 'L0_ffn_router_b', 'L0_ffn_expert_w',
        'L0_ffn_expert_b']
_OUTS = [((B, S, D), 'float32')]


def alibi_rows():
    import numpy as np
    slopes = 2.0 ** (np.arange(H) - 8)
    q_aug = np.zeros((HALF - AUG, PAIRS, S), np.float32)
    i = np.arange(S)
    q_aug[0], q_aug[1], q_aug[2] = 1.0, i % 256, i - i % 256
    k_aug = np.zeros((2, P, PAIRS, 2, JP), np.float32)
    for h in range(H):
        s = h % 2
        rows = k_aug[:, s * HALF + AUG:(s + 1) * HALF, h // 2, s, 0:J]
        rows[:, 0] = -slopes[h] * np.arange(J)
        rows[:, 1:3] = slopes[h]
        rows[1, 3:6] = 1.0
    bf16 = np.dtype("bfloat16")
    return q_aug.astype(bf16), k_aug.astype(bf16)


def kernel(**inputs):
    import numpy as _np
    import concourse.bacc as _bacc
    from concourse import mybir as _mybir
    from concourse.bass_utils import run_bass_kernel_spmd as _run

    nc = _bacc.Bacc("TRN2", target_bir_lowering=False, num_devices=1)
    arrays, args = {}, []

    def take(name, a):
        arrays[f"in_{name}_dram"] = a
        args.append(nc.dram_tensor(f"in_{name}_dram", a.shape, _mybir.dt.from_np(a.dtype), kind="ExternalInput").ap())

    for name in _INS:
        take(name, _np.ascontiguousarray(inputs[name]))
    for name, a in zip(("q_aug", "k_aug"), alibi_rows()):
        take(name, a)
    for i, (shape, dtype) in enumerate(_OUTS):
        dt = _mybir.dt.from_np(_np.dtype(dtype))
        args.append(nc.dram_tensor(f"out_{i}_dram", shape, dt, kind="ExternalOutput").ap())
    program(nc, *args)
    r = _run(nc, [arrays], core_ids=[0])
    got = tuple(r.results[0][f"out_{i}_dram"] for i in range(len(_OUTS)))
    return got[0]
```

```python
import concourse.bass as bass
from concourse import mybir
from contextlib import ExitStack

B, S, D = 4, 512, 128
J = 154
H = 16
DK = D // H
E = 8
P = 128
T = S // P
JM = P
JT = J - JM
JP = JM + 32
G = 4
R = H // G
PAIRS = H // 2
HALF = P // 2
EPS = 1e-5
QSCALE = float(DK) ** -0.5

K_PART = (0, 0, 0, 1, 1, 2)
Q_PART = (0, 1, 2, 0, 1, 0)
ROWS = DK * len(K_PART)
AUG = 2 * ROWS
MAXROW = AUG + 3
COPIES = 3 * E

ORDER = (
    ("stats1", 0, 0), ("rstd1", 0, 0), ("scores", 1, 0), ("y1", 0, 0), ("y1T", 0, 0), ("scores", 1, 1), ("values", 1, 0),
    ("dist", 0, 0), ("weights", 0, 0), ("rowmax", 0, 0),
    ("scores", 1, 2), ("values", 1, 1), ("ab", 0, 0), ("sub", 0, 0), ("keys", 0, 0), ("scores", 1, 3), ("values", 1, 2), ("self", 0, 0),
    ("values", 1, 3), ("gather", 0, 0), ("rstd2", 0, 0), ("divide", 1, 0), ("divide", 1, 1), ("y2", 0, 0), ("y2T", 0, 0), ("query", 0, 0), ("aoT", 1, 0), ("wo", 1, 0),
    ("rstd3", 1, 0), ("y3", 1, 0), ("y3T", 1, 0), ("route", 1, 0), ("mask", 1, 0),
    ("maxima", 0, 0), ("maxima", 0, 1), ("maxima", 0, 2), ("maxima", 0, 3), ("mcat", 0, 0), ("mT", 0, 0),
    ("select", 1, 0), ("experts", 1, 0), ("fT", 1, 0), ("store", 1, 0),
)
TURNS = B + 1
ONCE = ("weights", "keys")


def walk(steps):
    for turn in range(TURNS):
        for name, behind, k in ORDER:
            b = turn - behind
            if name in steps and 0 <= b < (1 if name in ONCE else B):
                steps[name](b, k)


def program(nc, x, ctx, gamma, Wq, bq, Wk, bk, Wv, bv, Wo, bo, rw, rb, ew, eb, q_aug, k_aug, part_rows, out):
    F32, BF16 = mybir.dt.float32, mybir.dt.bfloat16
    ALU, ACT, AX = mybir.AluOpType, mybir.ActivationFunctionType, mybir.AxisListType
    with ExitStack() as stack:
        def sb(name, shape, dtype=F32):
            return stack.enter_context(nc.sbuf_tensor(name, shape, dtype))

        def sem(name):
            return stack.enter_context(nc.semaphore(name))

        bank = [stack.enter_context(nc.psum_tensor(f"bank{i}", [P, S], F32)) for i in range(8)]
        ST = bank[0:2]
        MX = bank[2:4]
        YV = bank[4]
        YM = bank[5]
        A0 = bank[6]
        A1 = bank[7]

        ident = sb("ident", [P, P])
        ident16 = sb("ident16", [P, P], BF16)
        ones = sb("ones", [P, P])
        ones16 = sb("ones16", [P, P], BF16)
        thirty_second = sb("thirty_second", [P, 1])
        minus_half = sb("minus_half", [P, T])
        earlier = sb("earlier", [P, E, E])
        gam = sb("gam", [P, 1])
        gam2 = sb("gam2", [P, 1])
        gneg = sb("gneg", [P, 1])
        sgn = sb("sgn", [P, 1])
        wraw = sb("wraw", [P, 4, P])
        wT = sb("wT", [P, 4, P])
        ewraw = sb("ewraw", [P, E, P])
        ewT = sb("ewT", [P, E, P])
        rwraw = sb("rwraw", [P, P])
        rwT = sb("rwT", [P, E])
        ebraw = sb("ebraw", [COPIES, P])
        ebr = sb("ebr", [COPIES, 2, P])
        ebpart = sb("ebpart", [COPIES, 3, P], BF16)
        partsel = sb("partsel", [COPIES, 3])
        ebsum = sb("ebsum", [COPIES, 2, P], BF16)
        ebias = sb("ebias", [P, P], BF16)
        bqc = sb("bqc", [P, 1])
        bqs = sb("bqs", [P, 1])
        bkc = sb("bkc", [P, 1])
        bvb = sb("bvb", [P, P])
        bob = sb("bob", [P, P])
        rbb = sb("rbb", [P, E])
        ctx_m = sb("ctx_m", [P, B, D])
        ctx_t = sb("ctx_t", [32, B, D])
        ctxT = sb("ctxT", [P, B, JP])
        kf = sb("kf", [P, B, J])
        kr = sb("kr", [P, B, J])
        kpart = sb("kpart", [P, 3, B, JP], BF16)
        kA = sb("kA", [P, 2, PAIRS, JP], BF16)
        kB = sb("kB", [P, 2, PAIRS, JP], BF16)
        vm = sb("vm", [P, B, H, 32])
        vt = sb("vt", [P, B, R, P])

        xs = sb("xs", [P, B, T, D])
        st1 = sb("st1", [P, T, 6])
        mv1 = sb("mv1", [P, T, 2])
        ve1 = sb("ve1", [P, T])
        rs1 = sb("rs1", [P, T])
        y1 = sb("y1", [P, T, D])
        y1T = sb("y1T", [P, S])
        y1Tg = sb("y1Tg", [P, S])
        nsq = sb("nsq", [P, T])
        nsr = sb("nsr", [P, T])
        nst = sb("nst", [P, T])
        snsq = sb("snsq", [P, T])
        sqp = sb("sqp", [P, T, P], BF16)
        sqT = sb("sqT", [P, S], BF16)
        rm = sb("rm", [P, T])
        rma = sb("rma", [P, T])
        rmb = sb("rmb", [P, T])
        diag = sb("diag", [P, T, P])
        ab = sb("ab", [P, S])
        w = sb("w", [P, T, S])
        oT = sb("oT", [P, S])
        dn = sb("dn", [P, S])
        rd1 = sb("rd1", [P, T])
        x1 = sb("x1", [P, T, D])
        st2 = sb("st2", [P, T, 6])
        mv2 = sb("mv2", [P, T, 2])
        ve2 = sb("ve2", [P, T])
        rs2 = sb("rs2", [P, T])
        y2 = sb("y2", [P, T, D])
        y2T = sb("y2T", [P, S])
        qf = sb("qf", [P, S])
        qr = sb("qr", [P, S])
        qpart = sb("qpart", [P, 3, S], BF16)
        nm = sb("nm", [P, T, H])
        nmr = sb("nmr", [P, T, H])
        mcat = sb("mcat", [P, T, 3, H], BF16)
        mT = sb("mT", [3 * H, S], BF16)
        qs = sb("qs", [P, 2, PAIRS, S], BF16)
        x1b = sb("x1b", [P, 2, T, D])
        PT_RING = 2 * (G + 1)
        pt = sb("pt", [P, PT_RING, S])
        pvs = sb("pvs", [P, 2, S])
        rd2 = sb("rd2", [P, T, PAIRS])
        ao = sb("ao", [P, T, P])
        aoT = sb("aoT", [P, S])
        x2 = sb("x2", [P, 2, T, D])
        st3 = sb("st3", [P, T, 6])
        mv3 = sb("mv3", [P, T, 2])
        ve3 = sb("ve3", [P, T])
        rs3 = sb("rs3", [P, T])
        y3 = sb("y3", [P, T, D])
        y3T = sb("y3T", [P, S])
        lg = sb("lg", [P, T, E])
        cmp_eq = sb("cmp_eq", [P, T, E, E])
        cmp_gt = sb("cmp_gt", [P, T, E, E])
        rank = sb("rank", [P, T, E])
        maskp = sb("maskp", [P, T, P], BF16)
        maskT16 = sb("maskT16", [P, S], BF16)
        mask_all = sb("mask_all", [P, E, S], BF16)
        ym = sb("ym", [P, E, S])
        fT = sb("fT", [P, S])
        ob = sb("ob", [P, 2, T, D])

        k_scratch = nc.dram_tensor("k_scratch", [3, B, 2 * DK, PAIRS * JP], BF16, kind="Internal").ap()
        q_scratch = nc.dram_tensor("q_scratch", [3, 2 * DK, PAIRS * S], BF16, kind="Internal").ap()
        m_scratch = nc.dram_tensor("m_scratch", [3 * 2, PAIRS * S], BF16, kind="Internal").ap()
        e_scratch = nc.dram_tensor("e_scratch", [E, S], BF16, kind="Internal").ap()

        x_in = [sem(f"x_in{b}") for b in range(B)]
        gamma_in, weights_in, ctx_in = sem("gamma_in"), sem("weights_in"), sem("ctx_in")
        kaug_in, qaug_in = sem("kaug_in"), sem("qaug_in")
        k_out, q_out, m_out, e_out, e_in = sem("k_out"), sem("q_out"), sem("m_out"), sem("e_out"), sem("e_in")
        bias_ready, diag_done = sem("bias_ready"), sem("diag_done")
        zeroed, consts = sem("zeroed"), sem("consts")
        gamma_ready, bqs_ready = sem("gamma_ready"), sem("bqs_ready")
        setup_ps, setup_sb = sem("setup_ps"), sem("setup_sb")
        k_ready, v_ready = sem("k_ready"), sem("v_ready")
        kA_in, kB_in, qs_in, m_in, stored = sem("kA_in"), sem("kB_in"), sem("qs_in"), sem("m_in"), sem("stored")
        stats = [sem(f"stats{i}") for i in range(3)]
        rstd = [sem(f"rstd{i}") for i in range(3)]
        normed = [sem(f"normed{i}") for i in range(3)]
        y1T_ps, sqT_ps, y1T_sb, sq_ready = sem("y1T_ps"), sem("sqT_ps"), sem("y1T_sb"), sem("sq_ready")
        dist_ps, rm_ready, w_relu, rowmax = sem("dist_ps"), sem("rm_ready"), sem("w_relu"), sem("rowmax")
        diag_ready, ab_ps, ab_sb = sem("diag_ready"), sem("ab_ps"), sem("ab_sb")
        w_sub_v, w_sub_p, p_ready, self_ps, oT_sb, dn_sb = (
            sem("w_sub_v"), sem("w_sub_p"), sem("p_ready"), sem("self_ps"), sem("oT_sb"), sem("dn_sb"))
        gather_ps, x1_ready, x1b_ready = sem("gather_ps"), sem("x1_ready"), sem("x1b_ready")
        y2T_ps, y2T_sb, q_ps, qf_ready = sem("y2T_ps"), sem("y2T_sb"), sem("q_ps"), sem("qf_ready")
        q_hi, q_rest, q_mid, q_lo = sem("q_hi"), sem("q_rest"), sem("q_mid"), sem("q_lo")
        a_ps, maxed, mcat_ready, mT_ps, mT_sb = sem("a_ps"), sem("maxed"), sem("mcat_ready"), sem("mT_ps"), sem("mT_sb")
        st_ps, exps, pv_ps, pvs_sb = sem("st_ps"), sem("exps"), sem("pv_ps"), sem("pvs_sb")
        nd_ps, ao_ready, ao_ps, aoT_sb, wo_ps, x2_ready = (
            sem("nd_ps"), sem("ao_ready"), sem("ao_ps"), sem("aoT_sb"), sem("wo_ps"), sem("x2_ready"))
        y3T_ps, y3T_sb, lg_ps, mask_ready, mask_ps, mask_sb = (
            sem("y3T_ps"), sem("y3T_sb"), sem("lg_ps"), sem("mask_ready"), sem("mask_ps"), sem("mask_sb"))
        masked_v, masked_p, f_ps, fT_sb, fT_ps, out_ready = (
            sem("masked_v"), sem("masked_p"), sem("f_ps"), sem("fT_sb"), sem("fT_ps"), sem("out_ready"))
        act_own, dve_own, pool_own = sem("act_own"), sem("dve_own"), sem("pool_own")

        def own(engine, semaphore):
            n = [0]

            def done(ins):
                n[0] += 1
                ins.then_inc(semaphore, 1)

            def settle():
                engine.wait_ge(semaphore, n[0])
            return done, settle

        def tile(t):
            return slice(t * P, (t + 1) * P)

        def col16(tensor):
            return tensor[:, :].bitcast(BF16)

        ITEMS = G + 1
        RUNS = ((0, 3), (3, 2), (5, 1))
        ONE = 16
        W_LOADS = 13
        block = stack.enter_context(nc.Block())

        @block.sync
        def _(sp):
            def load(dst, src, s):
                sp.dma_start(dst, src).then_inc(s, ONE)

            load(xs[:, 0], x[0].rearrange("(t p) d -> p t d", p=P), x_in[0])
            load(gam[:, :], gamma.partition_broadcast(P), gamma_in)
            for i, m in enumerate((Wq, Wk, Wv)):
                load(wraw[:, i, :], m, weights_in)
            wo_view = Wo.rearrange("o (g f c) -> o f g c", g=G, f=2)
            for f in range(2):
                load(wraw[:, 3, f * HALF:(f + 1) * HALF].rearrange("o (g c) -> o g c", g=G), wo_view[:, f], weights_in)
            load(bqc[:, :], bq.rearrange("(p a) -> p a", a=1), weights_in)
            load(bkc[:, :], bk.rearrange("(p a) -> p a", a=1), weights_in)
            load(bvb[:, :], bv.partition_broadcast(P), weights_in)
            load(bob[:, :], bo.partition_broadcast(P), weights_in)
            load(rbb[:, :], rb.partition_broadcast(P), weights_in)
            load(ewraw[:, :, :], ew.rearrange("e h d -> h e d"), weights_in)
            load(partsel[:, :], part_rows, weights_in)
            load(ctx_m[:, :, :], ctx[:, 0:JM, :].rearrange("b j d -> j b d"), ctx_in)
            sp.wait_ge(zeroed, 2)
            load(ctx_t[0:JT, :, :], ctx[:, JM:J, :].rearrange("b j d -> j b d"), ctx_in)
            load(rwraw[0:E, :], rw, weights_in)
            for i in range(3):
                load(ebraw[i * E:(i + 1) * E, :], eb, ctx_in)
            load(kA[:, :, :, :], k_aug[0], kaug_in)
            load(kB[:, :, :, :], k_aug[1], kaug_in)
            for par in range(2):
                load(qs[AUG:P, par, :, :], q_aug, qaug_in)
            for b in range(1, B):
                load(xs[:, b], x[b].rearrange("(t p) d -> p t d", p=P), x_in[b])

            def stack_keys(stacks, b, s_in):
                for part, (r, n) in enumerate(RUNS):
                    for s in range(2):
                        row = s * ROWS + r * DK
                        src = k_scratch[part, b, s * DK:(s + 1) * DK, :].unsqueeze(0).broadcast_to([n, DK, PAIRS * JP])
                        load(stacks[row:row + n * DK, s, :, :].rearrange("p a j -> p (a j)"), src, s_in)

            def stats1(b, _):
                if b >= 1:
                    sp.wait_ge(maxed, b * T * PAIRS)
                    stack_keys(kA, b, kA_in)

            def keys(b, _):
                sp.wait_ge(k_ready, 1)
                for part in range(3):
                    for b in range(B):
                        load(k_scratch[part, b].rearrange("c (a j) -> a c j", a=PAIRS), kpart[:, part, b, :], k_out)
                sp.wait_ge(k_out, 3 * B * ONE)
                sp.wait_ge(kaug_in, 2 * ONE)
                stack_keys(kA, 0, kA_in)
                stack_keys(kB, 0, kB_in)

            def query(b, _):
                for part, got in enumerate((q_hi, q_mid, q_lo)):
                    sp.wait_ge(got, b + 1)
                    load(q_scratch[part].rearrange("c (a n) -> a c n", a=PAIRS), qpart[:, part, :], q_out)
                if b == 0:
                    sp.wait_ge(qaug_in, 2 * ONE)
                if b >= 2:
                    sp.wait_ge(st_ps, (b - 1) * R * ITEMS)
                sp.wait_ge(q_out, 3 * ONE * (b + 1))
                for r, n in RUNS:
                    for s in range(2):
                        row = s * ROWS + r * DK
                        load(qs[row:row + n * DK, b % 2, :, :].rearrange("p a n -> p (a n)"),
                             q_scratch[0:n, s * DK:(s + 1) * DK, :], qs_in)

            def divide(b, f):
                if f == 0 and b + 1 < B:
                    sp.wait_ge(st_ps, (b + 1) * R * ITEMS)
                    stack_keys(kB, b + 1, kB_in)

            def mT_(b, _):
                sp.wait_ge(mT_sb, b + 1)
                load(m_scratch.rearrange("r (a n) -> (r a) n", n=S), mT[:, :], m_out)
                sp.wait_ge(m_out, ONE * (b + 1))
                load(qs[MAXROW:MAXROW + 6, b % 2, :, :].rearrange("p a n -> p (a n)"), m_scratch, m_in)

            def mask(b, _):
                sp.wait_ge(mask_sb, b + 1)
                load(e_scratch, maskT16[0:E, :], e_out)
                if b >= 1:
                    sp.wait_ge(masked_v, b * E // 2)
                    sp.wait_ge(masked_p, b * E // 2)
                sp.wait_ge(e_out, ONE * (b + 1))
                load(mask_all[:, :, :], e_scratch.partition_broadcast(P), e_in)

            def store(b, _):
                sp.wait_ge(out_ready, b + 1)
                load(out[b].rearrange("(t p) d -> p t d", p=P), ob[:, b % 2], stored)

            walk({"stats1": stats1, "keys": keys, "query": query, "divide": divide, "mT": mT_, "mask": mask,
                  "store": store})
            sp.wait_ge(stored, ONE * B)

        @block.gpsimd
        def _(pool):
            done, settle = own(pool, pool_own)
            g = nc.gpsimd
            done(g.memset(ident[:, :], 0.0))
            done(g.memset(ident16[:, :], 0.0))
            g.memset(ctx_t[:, :, :], 0.0).then_inc(zeroed, 1)
            g.memset(rwraw[:, :], 0.0).then_inc(zeroed, 1)
            done(g.memset(minus_half[:, :], -0.5))
            settle()
            for m in (ident, ident16):
                g.affine_select(out=m[:, :], in_=m[:, :], compare_op=ALU.not_equal, fill=1.0, base=0,
                                pattern=[[-1, P]], channel_multiplier=1).then_inc(consts, 1)
            g.memset(sqp[:, :, :], 0.0).then_inc(consts, 1)
            g.memset(ones16[:, :], 1.0).then_inc(consts, 1)
            g.memset(ones[:, :], 1.0).then_inc(consts, 1)
            g.memset(thirty_second[:, :], 1.0 / 32).then_inc(consts, 1)
            pool.wait_ge(consts, 6)
            pool.wait_ge(gamma_in, ONE)
            done(g.tensor_scalar(gam2[:, :], gam[:, :], 2.0, 1.0, ALU.mult, ALU.mult))
            done(g.tensor_scalar(gneg[:, :], gam[:, :], -float(D), 1.0, ALU.mult, ALU.mult))
            done(g.tensor_scalar(rd1[:, 0:1], gam[:, :], 0.0, None, ALU.is_lt))
            settle()
            g.tensor_scalar(sgn[:, :], rd1[:, 0:1], 2.0, -1.0, ALU.mult, ALU.add).then_inc(gamma_ready, 1)
            pool.wait_ge(gamma_ready, 1)

            def norm(i, b, mv, ve, rs):
                pool.wait_ge(stats[i], b + 1)
                done(g.tensor_scalar(ve[:, :], mv[:, :, 1], EPS, 1.0, ALU.add, ALU.mult))
                settle()
                g.tensor_tensor(rs[:, :], ve[:, :], minus_half[:, :], ALU.pow).then_inc(rstd[i], 1)

            def rstd1(b, _):
                norm(0, b, mv1, ve1, rs1)
                pool.wait_ge(rstd[0], b + 1)
                if b >= 1:
                    pool.wait_ge(rowmax, b)
                    pool.wait_ge(w_relu, T * b)
                    pool.wait_ge(sqT_ps, b)
                done(g.tensor_tensor(nsr[:, :], rs1[:, :], rs1[:, :], ALU.mult))
                settle()
                done(g.tensor_tensor(nst[:, :], nsr[:, :], mv1[:, :, 1], ALU.mult))
                settle()
                done(g.tensor_scalar(nsq[:, :], nst[:, :], gneg[:, :], 1.0, ALU.mult, ALU.mult))
                settle()
                done(g.tensor_scalar(snsq[:, :], nsq[:, :], sgn[:, :], 1.0, ALU.mult, ALU.mult))
                done(g.tensor_copy(sqp[:, :, 0], nsq[:, :]))
                settle()
                done(g.tensor_tensor(nsr[:, :], nsq[:, :], sqp[:, :, 0], ALU.subtract))
                settle()
                done(g.tensor_copy(sqp[:, :, 1], nsr[:, :]))
                settle()
                done(g.tensor_tensor(nst[:, :], nsr[:, :], sqp[:, :, 1], ALU.subtract))
                settle()
                g.tensor_copy(sqp[:, :, 2], nst[:, :]).then_inc(sq_ready, 1)

            def weights(b, _):
                pool.wait_ge(weights_in, W_LOADS * ONE)
                pool.wait_ge(ctx_in, 5 * ONE)
                g.tensor_scalar(bqs[:, :], bqc[:, :], QSCALE, 1.0, ALU.mult, ALU.mult).then_inc(bqs_ready, 1)
                done(g.memset(earlier[:, :, :], 1.0))
                done(g.memset(maskp[:, :, :], 0.0))
                done(g.memset(ebias[:, :], 0.0))
                settle()
                g.affine_select(out=earlier[:, :, :], in_=earlier[:, :, :], compare_op=ALU.is_gt, fill=0.0, base=0,
                                pattern=[[1, E], [-1, E]], channel_multiplier=0).then_inc(consts, 1)
                done(g.tensor_copy(ebpart[:, 0, :], ebraw[:, :]))
                settle()
                done(g.tensor_tensor(ebr[:, 0, :], ebraw[:, :], ebpart[:, 0, :], ALU.subtract))
                settle()
                done(g.tensor_copy(ebpart[:, 1, :], ebr[:, 0, :]))
                settle()
                done(g.tensor_tensor(ebr[:, 1, :], ebr[:, 0, :], ebpart[:, 1, :], ALU.subtract))
                settle()
                done(g.tensor_copy(ebpart[:, 2, :], ebr[:, 1, :]))
                settle()
                for i in range(3):
                    done(g.tensor_scalar(ebpart[:, i, :], ebpart[:, i, :], partsel[:, i:i + 1], 1.0, ALU.mult, ALU.mult))
                settle()
                done(g.tensor_tensor(ebsum[:, 0, :], ebpart[:, 0, :], ebpart[:, 1, :], ALU.add))
                settle()
                g.tensor_tensor(ebias[0:COPIES, :], ebsum[:, 0, :], ebpart[:, 2, :], ALU.add).then_inc(bias_ready, 1)

            def sub(b, _):
                pool.wait_ge(ab_sb, b + 1)
                pool.wait_ge(w_relu, T * (b + 1))
                for t in range(0, T, 2):
                    g.tensor_tensor(w[:, t, :], w[:, t, :], ab[:, :], ALU.subtract).then_inc(w_sub_p, 1)

            def rstd2(b, _):
                norm(1, b, mv2, ve2, rs2)
                if b == 0:
                    pool.wait_ge(weights_in, W_LOADS * ONE)
                if b >= 2:
                    pool.wait_ge(x2_ready, b - 1)
                pool.wait_ge(x1_ready, b + 1)
                g.tensor_tensor(x1b[:, b % 2], x1[:, :, :], bob[:, :].unsqueeze(1).broadcast_to([P, T, D]),
                                ALU.add).then_inc(x1b_ready, 1)

            def rstd3(b, _):
                norm(2, b, mv3, ve3, rs3)

            def select(b, _):
                pool.wait_ge(e_in, ONE * (b + 1))
                pool.wait_ge(y3T_sb, b + 1)
                if b >= 1:
                    pool.wait_ge(f_ps, b)
                for e in range(1, E, 2):
                    g.tensor_tensor(ym[:, e, :], mask_all[:, e, :], y3T[:, :], ALU.mult).then_inc(masked_p, 1)

            walk({"rstd1": rstd1, "weights": weights, "sub": sub, "rstd2": rstd2, "rstd3": rstd3, "select": select})

        @block.scalar
        def _(act):
            copy = lambda dst, src: nc.scalar.activation(dst, src, ACT.Copy)

            def y1T_(b, _):
                if b == 0:
                    act.wait_ge(gamma_ready, 1)
                act.wait_ge(y1T_ps, b + 1)
                copy(y1T[:, :], A0[:, :]).then_inc(y1T_sb, 1)
                nc.scalar.activation(y1Tg[:, :], A0[:, :], ACT.Copy, scale=gam2[:, :]).then_inc(y1T_sb, 1)
                act.wait_ge(sqT_ps, b + 1)
                copy(sqT[:, :], col16(A1)[:, 0:S]).then_inc(y1T_sb, 1)

            def dist(b, _):
                for t in range(T):
                    act.wait_ge(rm_ready, T * b + t + 1)
                    nc.scalar.activation(w[:, t, :], (A0, A1)[t % 2][:, :], ACT.Relu, bias=snsq[:, t:t + 1],
                                         scale=sgn[:, :]).then_inc(w_relu, 1)

            def ab_(b, _):
                act.wait_ge(ab_ps, b + 1)
                copy(ab[:, :], A0[:, :]).then_inc(ab_sb, 1)

            def sub(b, _):
                for i, t in enumerate((1, 0, 3, 2)):
                    act.wait_ge(w_sub_p if t % 2 == 0 else w_sub_v, 2 * b + i // 2 + 1)
                    nc.scalar.activation(w[:, t, :], w[:, t, :], ACT.Exp, scale=sgn[:, :]).then_inc(p_ready, 1)

            def self_(b, _):
                act.wait_ge(self_ps, b + 1)
                copy(oT[:, :], A0[:, :]).then_inc(oT_sb, 1)

            def weights(b, _):
                act.wait_ge(setup_ps, 1)
                copy(wT[:, :, :], ST[0][:, :].rearrange("p (i n) -> p i n", i=4)).then_inc(setup_sb, 1)
                for i in range(2):
                    copy(ewT[:, 4 * i:4 * i + 4, :], (ST[1], MX[0])[i][:, :].rearrange("p (i n) -> p i n", i=4)).then_inc(setup_sb, 1)
                copy(rwT[:, :], YV[:, 0:E]).then_inc(setup_sb, 1)
                copy(ctxT[:, :, 0:JM], YM[:, :].rearrange("p (b j) -> p b j", b=B)).then_inc(setup_sb, 1)
                copy(ctxT[:, :, JM:JP], MX[1][:, 0:32 * B].rearrange("p (b j) -> p b j", b=B)).then_inc(setup_sb, 1)

            def keys(b, _):
                act.wait_ge(setup_ps, 2)
                act.wait_ge(weights_in, W_LOADS * ONE)
                for i in range(2):
                    nc.scalar.activation(kf[:, 2 * i:2 * i + 2, :],
                                         (ST[1], MX[0])[i][:, 0:2 * J].rearrange("p (b j) -> p b j", b=2),
                                         ACT.Identity, bias=bkc[:, :]).then_inc(setup_sb, 1)

            def y2T_(b, _):
                act.wait_ge(y2T_ps, b + 1)
                copy(y2T[:, :], A1[:, :]).then_inc(y2T_sb, 1)

            def query(b, _):
                act.wait_ge(q_ps, b + 1)
                if b == 0:
                    act.wait_ge(bqs_ready, 1)
                if b >= 1:
                    act.wait_ge(q_out, 3 * ONE * b)
                    act.wait_ge(q_lo, b)
                nc.scalar.activation(qf[:, :], A0[:, :], ACT.Identity, bias=bqs[:, :],
                                     scale=QSCALE).then_inc(qf_ready, 1)
                act.wait_ge(qf_ready, b + 1)
                copy(qpart[:, 0, :], qf[:, :]).then_inc(q_hi, 1)

            def mT_(b, _):
                act.wait_ge(mT_ps, b + 1)
                if b >= 1:
                    act.wait_ge(m_out, ONE * b)
                copy(mT[:, :], col16(MX[0])[0:3 * H, 0:S]).then_inc(mT_sb, 1)

            def scores(b, k):
                for i in range(ITEMS):
                    n = (b * R + k) * ITEMS + i
                    act.wait_ge(st_ps, n + 1)
                    if n >= PT_RING:
                        act.wait_ge(pv_ps, b * R + k - 1)
                    nc.scalar.activation(pt[:, n % PT_RING, :], ST[n % 2][:, :], ACT.Exp).then_inc(exps, 1)

            def values(b, k):
                if k % 2:
                    act.wait_ge(pv_ps, b * R + k + 1)
                    if b >= 1:
                        act.wait_ge(nd_ps, 2 * b)
                    copy(pvs[:, k // 2, :], YV[:, :]).then_inc(pvs_sb, 1)

            def aoT_(b, _):
                act.wait_ge(ao_ps, b + 1)
                copy(aoT[:, :], YM[:, :]).then_inc(aoT_sb, 1)

            def y3T_(b, _):
                act.wait_ge(y3T_ps, b + 1)
                if b >= 1:
                    act.wait_ge(masked_v, b * E // 2)
                    act.wait_ge(masked_p, b * E // 2)
                copy(y3T[:, :], YM[:, :]).then_inc(y3T_sb, 1)

            def mask(b, _):
                act.wait_ge(mask_ps, b + 1)
                if b >= 1:
                    act.wait_ge(e_out, ONE * b)
                    act.wait_ge(f_ps, b)
                copy(maskT16[:, :], col16(YM)[:, 0:S]).then_inc(mask_sb, 1)

            def fT_(b, _):
                act.wait_ge(f_ps, b + 1)
                copy(fT[:, :], YV[:, :]).then_inc(fT_sb, 1)

            walk({"y1T": y1T_, "dist": dist, "ab": ab_, "sub": sub, "self": self_, "weights": weights, "keys": keys,
                  "y2T": y2T_, "query": query, "mT": mT_, "scores": scores, "values": values, "aoT": aoT_,
                  "y3T": y3T_, "mask": mask, "fT": fT_})

        @block.vector
        def _(dve):
            done, settle = own(dve, dve_own)
            v = nc.vector

            def stats_of(i, src, st, mv):
                for t in range(T):
                    done(v.bn_stats(st[:, t, :], src(t)))
                settle()
                for t in range(T):
                    last = v.bn_aggr(mv[:, t, :], st[:, t, :])
                last.then_inc(stats[i], 1)

            def normalise(i, b, src, mv, rs, y):
                dve.wait_ge(stats[i], b + 1)
                dve.wait_ge(rstd[i], b + 1)
                for t in range(T):
                    last = v.tensor_scalar(y[:, t, :], src(t), mv[:, t, 0:1], rs[:, t:t + 1], ALU.subtract, ALU.mult)
                last.then_inc(normed[i], 1)

            def stats1(b, _):
                dve.wait_ge(x_in[b], ONE)
                if b >= 1:
                    dve.wait_ge(sq_ready, b)
                stats_of(0, lambda t: xs[:, b, t, :], st1, mv1)

            def y1_(b, _):
                if b >= 1:
                    dve.wait_ge(self_ps, b)
                normalise(0, b, lambda t: xs[:, b, t, :], mv1, rs1, y1)

            def dist(b, _):
                for t in range(T):
                    dve.wait_ge(dist_ps, T * b + t + 1)
                    v.tensor_reduce(rm[:, t:t + 1], (A0, A1)[t % 2][:, :], AX.X, ALU.max).then_inc(rm_ready, 1)

            def rowmax_(b, _):
                dve.wait_ge(rm_ready, T * (b + 1))
                dve.wait_ge(sq_ready, b + 1)
                done(v.scalar_tensor_tensor(out=rma[:, :], in0=rm[:, :], scalar=sgn[:, :], in1=snsq[:, :],
                                            op0=ALU.mult, op1=ALU.add))
                settle()
                v.tensor_scalar(rmb[:, :], rma[:, :], 0.0, None, ALU.max).then_inc(rowmax, 1)
                dve.wait_ge(rowmax, b + 1)
                for t in range(T):
                    last = v.tensor_scalar(diag[:, t, :], ident[:, :], rmb[:, t:t + 1], None, ALU.mult)
                last.then_inc(diag_ready, 1)

            def sub(b, _):
                dve.wait_ge(ab_sb, b + 1)
                dve.wait_ge(w_relu, T * (b + 1))
                for t in range(1, T, 2):
                    v.tensor_tensor(w[:, t, :], w[:, t, :], ab[:, :], ALU.subtract).then_inc(w_sub_v, 1)

            def self_(b, _):
                dve.wait_ge(self_ps, b + 1)
                v.tensor_copy(dn[:, :], A1[:, :]).then_inc(dn_sb, 1)

            def gather(b, _):
                dve.wait_ge(gather_ps, b + 1)
                done(v.reciprocal(rd1[:, :], A0[:, 0:T]))
                settle()
                if b >= 1:
                    dve.wait_ge(x1b_ready, b)
                for t in range(T):
                    last = v.scalar_tensor_tensor(out=x1[:, t, :], in0=A1[:, tile(t)], scalar=rd1[:, t:t + 1],
                                                  in1=xs[:, b, t, :], op0=ALU.mult, op1=ALU.add)
                last.then_inc(x1_ready, 1)
                dve.wait_ge(x1_ready, b + 1)
                stats_of(1, lambda t: x1[:, t, :], st2, mv2)

            def y2_(b, _):
                normalise(1, b, lambda t: x1[:, t, :], mv2, rs2, y2)

            def weights(b, _):
                done(v.memset(vm[:, :, :, :], 0.0))
                done(v.memset(vt[:, :, :, :], 0.0))
                done(v.memset(kpart[:, :, :, :], 0.0))
                settle()
                for s in range(2):
                    done(v.memset(vm[:, :, s::2, 16 * s + DK:16 * s + 2 * DK], 1.0))
                    for g in range(G):
                        c = 32 * g + 16 * s
                        done(v.memset(vt[32 * g:32 * g + JT, :, s::2, c + DK:c + 2 * DK], 1.0))

            def keys(b, _):
                dve.wait_ge(setup_sb, 8)
                dve.wait_ge(weights_in, W_LOADS * ONE)
                done(v.tensor_copy(kpart[:, 0, :, 0:J], kf[:, :, :]))
                settle()
                done(v.tensor_tensor(kr[:, :, :], kf[:, :, :], kpart[:, 0, :, 0:J], ALU.subtract))
                settle()
                done(v.tensor_copy(kpart[:, 1, :, 0:J], kr[:, :, :]))
                settle()
                v.tensor_tensor(kpart[:, 2, :, 0:J], kr[:, :, :], kpart[:, 1, :, 0:J], ALU.subtract).then_inc(k_ready, 1)
                for b in range(B):
                    val = YM[:, tile(b)].rearrange("p (a s d) -> p s a d", s=2, d=DK)
                    bias = bvb[:, :].rearrange("p (a s d) -> p s a d", s=2, d=DK)
                    for s in range(2):
                        v.tensor_tensor(vm[:, b, s::2, 16 * s:16 * s + DK], val[:, s], bias[:, s],
                                        ALU.add).then_inc(v_ready, 1)
                for g in range(G):
                    rows = slice(32 * g, 32 * g + JT)
                    val = YV[rows, 0:32 * B].rearrange("p (b a s d) -> p s b a d", b=B, s=2, d=DK)
                    bias = bvb[rows, 32 * g:32 * g + 32].rearrange("p (a s d) -> p s a d", s=2, d=DK)
                    for s in range(2):
                        c = 32 * g + 16 * s
                        v.tensor_tensor(vt[rows, :, s::2, c:c + DK], val[:, s],
                                        bias[:, s].unsqueeze(1).broadcast_to([JT, B, 2, DK]),
                                        ALU.add).then_inc(v_ready, 1)

            def query(b, _):
                dve.wait_ge(q_hi, b + 1)
                v.tensor_tensor(qr[:, :], qf[:, :], qpart[:, 0, :], ALU.subtract).then_inc(q_rest, 1)
                dve.wait_ge(q_rest, b + 1)
                v.tensor_copy(qpart[:, 1, :], qr[:, :]).then_inc(q_mid, 1)
                dve.wait_ge(q_mid, b + 1)
                v.tensor_tensor(qpart[:, 2, :], qr[:, :], qpart[:, 1, :], ALU.subtract).then_inc(q_lo, 1)

            def maxima(b, t):
                for a in range(PAIRS):
                    dve.wait_ge(a_ps, (b * T + t) * PAIRS + a + 1)
                    v.tensor_reduce(nm[:, t, 2 * a:2 * a + 2], MX[a % 2][:, 0:2 * J].rearrange("p (s j) -> p s j", s=2),
                                    AX.X, ALU.max, negate=True).then_inc(maxed, 1)

            def mcat_(b, _):
                neg = nm[:, :, :].rearrange("p t (a s) -> p t s a", s=2)
                rest = nmr[:, :, :].rearrange("p t (s a) -> p t s a", s=2)
                part = [mcat[:, :, i, :].rearrange("p t (s a) -> p t s a", s=2) for i in range(3)]
                dve.wait_ge(maxed, (b + 1) * T * PAIRS)
                done(v.tensor_copy(part[0], neg))
                settle()
                done(v.tensor_tensor(rest, neg, part[0], ALU.subtract))
                settle()
                done(v.tensor_copy(part[1], rest))
                settle()
                v.tensor_tensor(part[2], rest, part[1], ALU.subtract).then_inc(mcat_ready, 1)

            def divide(b, f):
                nd = YM[:, :].rearrange("p (t c x) -> p t c x", t=T, x=2 * DK)
                dve.wait_ge(nd_ps, 2 * b + f + 1)
                done(v.reciprocal(rd2[:, :, :], nd[:, :, :, DK]))
                settle()
                v.tensor_tensor(ao[:, :, f * HALF:(f + 1) * HALF].rearrange("p t (c d) -> p t c d", d=DK),
                                nd[:, :, :, 0:DK], rd2[:, :, :].unsqueeze(3).broadcast_to([P, T, PAIRS, DK]),
                                ALU.mult).then_inc(ao_ready, 1)

            def wo(b, _):
                dve.wait_ge(wo_ps, b + 1)
                dve.wait_ge(x1b_ready, b + 1)
                v.tensor_tensor(x2[:, b % 2], YV[:, :].rearrange("p (t d) -> p t d", t=T), x1b[:, b % 2],
                                ALU.add).then_inc(x2_ready, 1)
                dve.wait_ge(x2_ready, b + 1)
                stats_of(2, lambda t: x2[:, b % 2, t, :], st3, mv3)

            def y3_(b, _):
                normalise(2, b, lambda t: x2[:, b % 2, t, :], mv3, rs3, y3)

            def route(b, _):
                dve.wait_ge(lg_ps, b + 1)
                if b == 0:
                    dve.wait_ge(consts, 7)
                    dve.wait_ge(weights_in, W_LOADS * ONE)
                done(v.tensor_tensor(lg[:, :, :], YV[:, 0:T * E].rearrange("p (t e) -> p t e", t=T),
                                     rbb[:, :].unsqueeze(1).broadcast_to([P, T, E]), ALU.add))
                settle()
                other = lg[:, :, :].unsqueeze(2).broadcast_to([P, T, E, E])
                mine = lg[:, :, :].unsqueeze(3).broadcast_to([P, T, E, E])
                done(v.tensor_tensor(cmp_eq[:, :, :, :], other, mine, ALU.is_equal))
                done(v.tensor_tensor(cmp_gt[:, :, :, :], other, mine, ALU.is_gt))
                settle()
                done(v.tensor_tensor(cmp_eq[:, :, :, :], cmp_eq[:, :, :, :],
                                     earlier[:, :, :].unsqueeze(1).broadcast_to([P, T, E, E]), ALU.mult))
                settle()
                done(v.tensor_tensor(cmp_gt[:, :, :, :], cmp_gt[:, :, :, :], cmp_eq[:, :, :, :], ALU.add))
                settle()
                done(v.tensor_reduce(rank[:, :, :], cmp_gt[:, :, :, :], AX.X, ALU.add))
                settle()
                v.tensor_scalar(maskp[:, :, 0:COPIES].rearrange("p t (i e) -> p t i e", e=E),
                                rank[:, :, :].unsqueeze(2).broadcast_to([P, T, 3, E]), 1.5, None,
                                ALU.is_lt).then_inc(mask_ready, 1)

            def select(b, _):
                dve.wait_ge(e_in, ONE * (b + 1))
                dve.wait_ge(y3T_sb, b + 1)
                if b >= 1:
                    dve.wait_ge(f_ps, b)
                for e in range(0, E, 2):
                    v.tensor_tensor(ym[:, e, :], mask_all[:, e, :], y3T[:, :], ALU.mult).then_inc(masked_v, 1)

            def store(b, _):
                dve.wait_ge(fT_ps, b + 1)
                if b >= 2:
                    dve.wait_ge(stored, ONE * (b - 1))
                v.tensor_tensor(ob[:, b % 2], YM[:, :].rearrange("p (t d) -> p t d", t=T), x2[:, b % 2],
                                ALU.add).then_inc(out_ready, 1)

            walk({"stats1": stats1, "y1": y1_, "dist": dist, "rowmax": rowmax_, "sub": sub, "self": self_,
                  "gather": gather, "y2": y2_, "weights": weights, "keys": keys, "query": query, "maxima": maxima,
                  "mcat": mcat_, "divide": divide, "wo": wo, "y3": y3_, "route": route, "select": select, "store": store})

        @block.tensor
        def _(pe):
            mm = nc.tensor.matmul
            pe.wait_ge(consts, 6)

            def turn(bank_, src, id_=ident):
                for t in range(T):
                    last = nc.tensor.transpose(bank_[:, tile(t)], src(t), id_[:, :])
                return last

            def weights(b, _):
                pe.wait_ge(weights_in, W_LOADS * ONE)
                pe.wait_ge(ctx_in, 5 * ONE)
                turn(ST[0], lambda i: wraw[:, i, :])
                turn(ST[1], lambda i: ewraw[:, i, :])
                turn(MX[0], lambda i: ewraw[:, 4 + i, :])
                nc.tensor.transpose(YV[:, 0:P], rwraw[:, :], ident[:, :])
                turn(YM, lambda i: ctx_m[:, i, :])
                for i in range(B):
                    last = nc.tensor.transpose(MX[1][:, 32 * i:32 * i + 32], ctx_t[:, i, :], ident[0:32, 0:32])
                last.then_inc(setup_ps, 1)

            def keys(b, _):
                pe.wait_ge(setup_sb, 6)
                for i in range(2):
                    mm((ST[1], MX[0])[i][:, 0:2 * J], wT[:, 1, :], ctxT[:, 2 * i:2 * i + 2, 0:J], start=True, stop=True)
                for i in range(B):
                    mm(YM[:, tile(i)], ctxT[:, i, 0:JM], wT[:, 2, :], start=True, stop=True)
                for i in range(B):
                    for g in range(G):
                        last = mm(YV[32 * g:32 * g + 32, 32 * i:32 * i + 32], ctxT[:, i, JM:JP],
                                  wT[:, 2, 32 * g:32 * g + 32], start=True, stop=True)
                last.then_inc(setup_ps, 1)

            def y1T_(b, _):
                pe.wait_ge(normed[0], b + 1)
                if b >= 1:
                    pe.wait_ge(y2T_sb, b)
                    pe.wait_ge(qf_ready, b)
                turn(A0, lambda t: y1[:, t, :]).then_inc(y1T_ps, 1)
                pe.wait_ge(sq_ready, b + 1)
                turn(col16(A1), lambda t: sqp[:, t, :], ident16).then_inc(sqT_ps, 1)

            def dist(b, _):
                pe.wait_ge(y1T_sb, 3 * (b + 1))
                for t in range(T):
                    if t >= 2:
                        pe.wait_ge(w_relu, T * b + t - 1)
                    mm((A0, A1)[t % 2][:, :], y1T[:, tile(t)], y1Tg[:, :], start=True, stop=False)
                    mm((A0, A1)[t % 2][:, :], ones16[:, :], sqT[:, :], start=False, stop=True).then_inc(dist_ps, 1)

            def ab_(b, _):
                pe.wait_ge(diag_ready, b + 1)
                pe.wait_ge(w_relu, T * (b + 1))
                mm(A0[:, :], ones[:, :], diag[:, :, :], start=True, stop=True).then_inc(ab_ps, 1)

            def self_(b, _):
                for i, t in enumerate((1, 0, 3, 2)):
                    pe.wait_ge(p_ready, T * b + i + 1)
                    mm(A0[:, :], y1[:, t, :], w[:, t, :], start=(i == 0), stop=(i == T - 1))
                for t in range(T):
                    last = mm(A1[32 * t:32 * t + 32, :], ones[:, 0:32], w[:, t, :], start=True, stop=True)
                last.then_inc(self_ps, 1)

            def gather(b, _):
                pe.wait_ge(oT_sb, b + 1)
                pe.wait_ge(dn_sb, b + 1)
                turn(A1, lambda t: oT[:, tile(t)])
                for t in range(T):
                    last = mm(A0[:, t:t + 1], dn[:, tile(t)], thirty_second[:, :], start=True, stop=True)
                last.then_inc(gather_ps, 1)

            def y2T_(b, _):
                pe.wait_ge(normed[1], b + 1)
                turn(A1, lambda t: y2[:, t, :]).then_inc(y2T_ps, 1)

            def query(b, _):
                pe.wait_ge(y2T_sb, b + 1)
                if b == 0:
                    pe.wait_ge(setup_sb, 6)
                mm(A0[:, :], wT[:, 0, :], y2T[:, :], start=True, stop=True).then_inc(q_ps, 1)

            def maxima(b, t):
                if t == 0:
                    pe.wait_ge(kA_in, 6 * ONE * (b + 1))
                    pe.wait_ge(qs_in, 6 * ONE * (b + 1))
                    if b == 0:
                        pe.wait_ge(setup_sb, 8)
                    if b >= 1:
                        pe.wait_ge(mT_sb, b)
                for a in range(PAIRS):
                    n = (b * T + t) * PAIRS + a
                    if n >= 2:
                        pe.wait_ge(maxed, n - 1)
                    mm(MX[a % 2][:, 0:2 * J], qs[:, b % 2, a, tile(t)], kA[:, :, a, 0:J],
                       start=True, stop=True).then_inc(a_ps, 1)

            def mT_(b, _):
                pe.wait_ge(mcat_ready, b + 1)
                turn(col16(MX[0])[0:3 * H], lambda t: mcat[:, t, :, :].rearrange("p i h -> p (i h)"),
                     ident16).then_inc(mT_ps, 1)

            def scores(b, k):
                if k == 0:
                    pe.wait_ge(kB_in, 6 * ONE * (b + 1))
                    pe.wait_ge(m_in, ONE * (b + 1))
                for i in range(ITEMS):
                    n = (b * R + k) * ITEMS + i
                    if n >= 2:
                        pe.wait_ge(exps, n - 1)
                    if i < G:
                        h = R * i + k
                        last = mm(ST[n % 2][:, :], kB[:, h % 2, h // 2, 0:JM], qs[:, b % 2, h // 2, :],
                                  start=True, stop=True)
                    else:
                        for g in range(G):
                            h = R * g + k
                            last = mm(ST[n % 2][32 * g:32 * g + 32, :], kB[:, h % 2, h // 2, JM:JP],
                                      qs[:, b % 2, h // 2, :], start=True, stop=True)
                    last.then_inc(st_ps, 1)

            def values(b, k):
                n = (b * R + k) * ITEMS
                if k == 0 and b == 0:
                    pe.wait_ge(v_ready, 2 * B + 2 * G)
                if k == 0 and b >= 1:
                    pe.wait_ge(fT_sb, b)
                if k == 2:
                    pe.wait_ge(pvs_sb, 2 * b + 1)
                pe.wait_ge(exps, n + ITEMS)
                for g in range(G):
                    mm(YV[32 * g:32 * g + 32, :], vm[:, b, R * g + k, :], pt[:, (n + g) % PT_RING, :],
                       start=(k % 2 == 0), stop=False, skip_group_check=True)
                mm(YV[:, :], vt[:, b, k, :], pt[:, (n + G) % PT_RING, :], start=False, stop=(k % 2 == 1),
                   skip_group_check=True).then_inc(pv_ps, 1)

            def divide(b, f):
                pe.wait_ge(pvs_sb, 2 * b + f + 1)
                if f == 0 and b >= 1:
                    pe.wait_ge(out_ready, b)
                if f == 1:
                    pe.wait_ge(ao_ready, 2 * b + 1)
                turn(YM, lambda t: pvs[:, f, tile(t)]).then_inc(nd_ps, 1)

            def aoT_(b, _):
                pe.wait_ge(ao_ready, 2 * b + 2)
                turn(YM, lambda t: ao[:, t, :]).then_inc(ao_ps, 1)

            def wo(b, _):
                pe.wait_ge(aoT_sb, b + 1)
                for t in range(T):
                    last = mm(YV[:, tile(t)], aoT[:, tile(t)], wT[:, 3, :], start=True, stop=True)
                last.then_inc(wo_ps, 1)

            def y3T_(b, _):
                pe.wait_ge(normed[2], b + 1)
                turn(YM, lambda t: y3[:, t, :]).then_inc(y3T_ps, 1)

            def route(b, _):
                pe.wait_ge(y3T_sb, b + 1)
                for t in range(T):
                    last = mm(YV[:, t * E:(t + 1) * E], y3T[:, tile(t)], rwT[:, :], start=True, stop=True)
                last.then_inc(lg_ps, 1)

            def mask(b, _):
                pe.wait_ge(mask_ready, b + 1)
                turn(col16(YM), lambda t: maskp[:, t, :], ident16).then_inc(mask_ps, 1)

            def experts(b, _):
                pe.wait_ge(mask_sb, b + 1)
                if b == 0:
                    pe.wait_ge(bias_ready, 1)
                mm(YV[:, :], ebias[:, :], maskT16[:, :], start=True, stop=False)
                for e in range(E):
                    pe.wait_ge(masked_p if e % 2 else masked_v, b * E // 2 + e // 2 + 1)
                    last = mm(YV[:, :], ewT[:, e, :], ym[:, e, :], start=False, stop=(e == E - 1))
                last.then_inc(f_ps, 1)

            def fT_(b, _):
                pe.wait_ge(fT_sb, b + 1)
                turn(YM, lambda t: fT[:, tile(t)]).then_inc(fT_ps, 1)

            walk({"y1T": y1T_, "dist": dist, "ab": ab_, "self": self_, "gather": gather, "weights": weights,
                  "keys": keys, "y2T": y2T_, "query": query, "maxima": maxima, "mT": mT_, "scores": scores,
                  "values": values, "divide": divide, "aoT": aoT_, "wo": wo, "y3T": y3T_, "route": route,
                  "mask": mask, "experts": experts, "fT": fT_})


_INS = ['x', 'ctx_1024', 'L0_attn_gamma', 'L0_xattn_Wq', 'L0_xattn_bq', 'L0_xattn_Wk', 'L0_xattn_bk', 'L0_xattn_Wv',
        'L0_xattn_bv', 'L0_xattn_Wo', 'L0_xattn_bo', 'L0_ffn_router_w', 'L0_ffn_router_b', 'L0_ffn_expert_w',
        'L0_ffn_expert_b']
_OUTS = [((B, S, D), 'float32')]


def alibi_rows():
    import numpy as np
    slopes = 2.0 ** (np.arange(H) - 8)
    q_aug = np.zeros((P - AUG, PAIRS, S), np.float32)
    i = np.arange(S)
    q_aug[0], q_aug[1], q_aug[2] = 1.0, i % 256, i - i % 256
    k_aug = np.zeros((2, P, 2, PAIRS, JP), np.float32)
    for h in range(H):
        a, s = h // 2, h % 2
        k_aug[:, AUG, s, a, 0:J] = -slopes[h] * np.arange(J)
        k_aug[:, AUG + 1:AUG + 3, s, a, 0:J] = slopes[h]
        k_aug[1, MAXROW + s:MAXROW + 6:2, s, a, 0:J] = 1.0
    part_rows = np.repeat(np.eye(3), E, axis=0).astype(np.float32)
    bf16 = np.dtype("bfloat16")
    return q_aug.astype(bf16), k_aug.astype(bf16), part_rows


def kernel(**inputs):
    import numpy as _np
    import concourse.bacc as _bacc
    from concourse import mybir as _mybir
    from concourse.bass_utils import run_bass_kernel_spmd as _run

    nc = _bacc.Bacc("TRN2", target_bir_lowering=False, num_devices=1)
    arrays, args = {}, []

    def take(name, a):
        arrays[f"in_{name}_dram"] = a
        args.append(nc.dram_tensor(f"in_{name}_dram", a.shape, _mybir.dt.from_np(a.dtype), kind="ExternalInput").ap())

    for name in _INS:
        take(name, _np.ascontiguousarray(inputs[name]))
    for name, a in zip(("q_aug", "k_aug", "part_rows"), alibi_rows()):
        take(name, a)
    for i, (shape, dtype) in enumerate(_OUTS):
        dt = _mybir.dt.from_np(_np.dtype(dtype))
        args.append(nc.dram_tensor(f"out_{i}_dram", shape, dt, kind="ExternalOutput").ap())
    program(nc, *args)
    r = _run(nc, [arrays], core_ids=[0])
    got = tuple(r.results[0][f"out_{i}_dram"] for i in range(len(_OUTS)))
    return got[0]
```

```python
import concourse.bass as bass
from concourse import mybir
from contextlib import ExitStack

B, S, D = 4, 512, 128
J = 154
H = 16
DK = D // H
E = 8
P = 128
T = S // P
JM = P
JT = J - JM
JP = JM + 32
G = 4
R = H // G
PAIRS = H // 2
HALF = P // 2
EPS = 1e-5
QSCALE = float(DK) ** -0.5

K_PART = (0, 1, 2, 0, 1, 0)
Q_PART = (0, 0, 0, 1, 1, 2)
COPY = len(K_PART)
ROWS = DK * COPY
AUG = 2 * ROWS
MAXROW = AUG + 3
COPIES = 3 * E

ORDER = {
    "sync": """
        query:0 keys:0 more_keys:0 stats1:1 mT:0 query:1 stats1:2 divide:0.0 mT:1 mask:0 query:2 divide:1.0
        stats1:3 mT:2 mask:1 query:3 store:0 store:1 divide:2.0 mT:3 mask:2 mask:3 store:2 store:3
    """,
    "gpsimd": """
        rstd1:0 sub:0 rstd1:1 weights:0 rstd2:0 sub:1 rstd1:2 rstd2:1 sub:2 rstd1:3 rstd3:0 rstd2:2 select:0
        sub:3 rstd3:1 rstd2:3 select:1 rstd3:2 select:2 rstd3:3 select:3
    """,
    "scalar": """
        y1T:0 dist:0 ab:0 sub:0 self:0 weights:0 y2T:0 keys:0 query:0 y1T:1 dist:1 ab:1 sub:1 mT:0 self:1
        scores:0.0 scores:0.1 scores:0.2 scores:0.3 scores:0.4 scores:0.5 y2T:1 query:1 y1T:2 values:0.1 dist:2
        scores:0.6 scores:0.7 scores:0.8 scores:0.9 scores:0.10 ab:2 scores:0.11 sub:2 values:0.3 aoT:0 self:2
        y3T:0 mT:1 mask:0 scores:1.0 scores:1.1 scores:1.2 scores:1.3 y2T:2 query:2 scores:1.4 fT:0 y1T:3
        scores:1.5 scores:1.6 dist:3 scores:1.7 scores:1.8 scores:1.9 values:1.1 ab:3 scores:1.10 scores:1.11
        sub:3 values:1.3 aoT:1 self:3 mT:2 y3T:1 mask:1 scores:2.0 scores:2.1 scores:2.2 scores:2.3 scores:2.4
        y2T:3 query:3 fT:1 scores:2.5 scores:2.6 scores:2.7 values:2.1 scores:2.8 scores:2.9 scores:2.10
        scores:2.11 values:2.3 aoT:2 y3T:2 mT:3 mask:2 scores:3.0 scores:3.1 scores:3.2 scores:3.3 scores:3.4
        scores:3.5 fT:2 scores:3.6 values:3.1 scores:3.7 scores:3.8 scores:3.9 scores:3.10 scores:3.11
        values:3.3 aoT:3 y3T:3 mask:3 fT:3
    """,
    "vector": """
        stats1:0 y1:0 dist:0 rowmax:0 stats1:1 sub:0 weights:0 self:0 gather:0 y1:1 y2:0 query:0 keys:0 dist:1
        rowmax:1 maxima:0.0 maxima:0.1 maxima:0.2 maxima:0.3 maxima:0.4 maxima:0.5 maxima:0.6 maxima:0.7
        maxima:0.8 maxima:0.9 maxima:0.10 mcat:0 sub:1 stats1:2 self:1 y1:2 gather:1 stats1:3 y2:1 query:1
        dist:2 maxima:1.0 maxima:1.1 rowmax:2 maxima:1.2 maxima:1.3 maxima:1.4 maxima:1.5 maxima:1.6 sub:2
        divide:0.0 maxima:1.7 divide:0.1 maxima:1.8 maxima:1.9 wo:0 maxima:1.10 mcat:1 y3:0 self:2 route:0
        gather:2 y2:2 select:0 query:2 y1:3 dist:3 rowmax:3 maxima:2.0 maxima:2.1 maxima:2.2 maxima:2.3
        maxima:2.4 store:0 maxima:2.5 divide:1.0 sub:3 maxima:2.6 maxima:2.7 divide:1.1 maxima:2.8 maxima:2.9
        wo:1 maxima:2.10 mcat:2 y3:1 self:3 route:1 gather:3 y2:3 select:1 query:3 maxima:3.0 maxima:3.1
        maxima:3.2 maxima:3.3 store:1 maxima:3.4 divide:2.0 maxima:3.5 maxima:3.6 divide:2.1 maxima:3.7
        maxima:3.8 wo:2 maxima:3.9 maxima:3.10 y3:2 mcat:3 route:2 select:2 store:2 divide:3.0 divide:3.1 wo:3
        y3:3 route:3 select:3 store:3
    """,
    "tensor": """
        y1T:0 dist:0 weights:0 ab:0 self:0 gather:0 keys:0 y2T:0 query:0 y1T:1 dist:1 maxima:0.0 maxima:0.1
        maxima:0.2 maxima:0.3 maxima:0.4 maxima:0.5 maxima:0.6 maxima:0.7 maxima:0.8 maxima:0.9 maxima:0.10 ab:1
        mT:0 self:1 gather:1 scores:0.0 scores:0.1 scores:0.2 scores:0.3 scores:0.4 scores:0.5 y2T:1 scores:0.6
        query:1 values:0.0 y1T:2 values:0.1 dist:2 maxima:1.0 maxima:1.1 scores:0.7 divide:0.0 maxima:1.2
        scores:0.8 ab:2 scores:0.9 maxima:1.3 maxima:1.4 maxima:1.5 scores:0.10 maxima:1.6 scores:0.11
        values:0.2 maxima:1.7 values:0.3 divide:0.1 maxima:1.8 aoT:0 maxima:1.9 wo:0 maxima:1.10 self:2 y3T:0
        mT:1 route:0 gather:2 mask:0 scores:1.0 scores:1.1 scores:1.2 scores:1.3 y2T:2 query:2 scores:1.4
        experts:0 y1T:3 scores:1.5 values:1.0 scores:1.6 dist:3 maxima:2.0 values:1.1 maxima:2.1 scores:1.7
        maxima:2.2 fT:0 maxima:2.3 scores:1.8 maxima:2.4 scores:1.9 ab:3 maxima:2.5 scores:1.10 maxima:2.6
        divide:1.0 scores:1.11 values:1.2 values:1.3 maxima:2.7 divide:1.1 maxima:2.8 aoT:1 maxima:2.9 wo:1
        maxima:2.10 self:3 mT:2 y3T:1 route:1 gather:3 mask:1 scores:2.0 scores:2.1 scores:2.2 scores:2.3
        scores:2.4 y2T:3 scores:2.5 query:3 experts:1 values:2.0 values:2.1 maxima:3.0 scores:2.6 maxima:3.1
        scores:2.7 maxima:3.2 scores:2.8 fT:1 maxima:3.3 scores:2.9 maxima:3.4 scores:2.10 divide:2.0
        scores:2.11 maxima:3.5 values:2.2 values:2.3 maxima:3.6 divide:2.1 maxima:3.7 aoT:2 maxima:3.8 wo:2
        maxima:3.9 maxima:3.10 y3T:2 mT:3 route:2 mask:2 scores:3.0 scores:3.1 scores:3.2 scores:3.3 scores:3.4
        scores:3.5 experts:2 scores:3.6 fT:2 values:3.0 values:3.1 scores:3.7 divide:3.0 scores:3.8 scores:3.9
        scores:3.10 scores:3.11 values:3.2 values:3.3 divide:3.1 aoT:3 wo:3 y3T:3 route:3 mask:3 experts:3 fT:3
    """,
}


def walk(engine, steps):
    for item in ORDER[engine].split():
        name, _, at = item.partition(":")
        b, _, k = at.partition(".")
        steps[name](int(b), int(k or 0))


def program(nc, x, ctx, gamma, Wq, bq, Wk, bk, Wv, bv, Wo, bo, rw, rb, ew, eb, q_aug, k_aug, part_rows, out):
    F32, BF16 = mybir.dt.float32, mybir.dt.bfloat16
    ALU, ACT, AX = mybir.AluOpType, mybir.ActivationFunctionType, mybir.AxisListType
    with ExitStack() as stack:
        def sb(name, shape, dtype=F32):
            return stack.enter_context(nc.sbuf_tensor(name, shape, dtype))

        def sem(name):
            return stack.enter_context(nc.semaphore(name))

        bank = [stack.enter_context(nc.psum_tensor(f"bank{i}", [P, S], F32)) for i in range(8)]
        ST = bank[0:2]
        MX = bank[2:4]
        YV = bank[4]
        YM = bank[5]
        A0 = bank[6]
        A1 = bank[7]

        ident = sb("ident", [P, P])
        ident16 = sb("ident16", [P, P], BF16)
        ones = sb("ones", [P, P])
        ones16 = sb("ones16", [P, P], BF16)
        thirty_second = sb("thirty_second", [P, 1])
        warm = sb("warm", [P, 1])
        minus_half = sb("minus_half", [P, T])
        earlier = sb("earlier", [P, E, E])
        gam = sb("gam", [P, 1])
        gam2 = sb("gam2", [P, 1])
        gneg = sb("gneg", [P, 1])
        sgn = sb("sgn", [P, 1])
        wraw = sb("wraw", [P, 4, P])
        wT = sb("wT", [P, 4, P])
        ewraw = sb("ewraw", [P, E, P])
        ewT = sb("ewT", [P, E, P])
        rwraw = sb("rwraw", [P, P])
        rwT = sb("rwT", [P, E])
        ebraw = sb("ebraw", [COPIES, P])
        ebr = sb("ebr", [COPIES, 2, P])
        ebpart = sb("ebpart", [COPIES, 3, P], BF16)
        partsel = sb("partsel", [COPIES, 3])
        ebsum = sb("ebsum", [COPIES, 2, P], BF16)
        ebias = sb("ebias", [P, P], BF16)
        bqc = sb("bqc", [P, 1])
        bqs = sb("bqs", [P, 1])
        bkc = sb("bkc", [P, 1])
        bvb = sb("bvb", [P, P])
        bob = sb("bob", [P, P])
        rbb = sb("rbb", [P, E])
        ctx_m = sb("ctx_m", [P, B, D])
        ctx_t = sb("ctx_t", [32, B, D])
        ctxT = sb("ctxT", [P, B, JP])
        kf = sb("kf", [P, B, J])
        kr = sb("kr", [P, B, J])
        kpart = sb("kpart", [P, 3, B, JP], BF16)
        kA = sb("kA", [P, 2, PAIRS, JP], BF16)
        kB = sb("kB", [P, 2, PAIRS, JP], BF16)
        vm = sb("vm", [P, B, H, 32])
        vt = sb("vt", [P, B, R, P])

        xs = sb("xs", [P, B, T, D])
        st1 = sb("st1", [P, T, 6])
        mv1 = sb("mv1", [P, T, 2])
        ve1 = sb("ve1", [P, T])
        rs1 = sb("rs1", [P, T])
        y1 = sb("y1", [P, T, D])
        y1T = sb("y1T", [P, S])
        y1Tg = sb("y1Tg", [P, S])
        nsq = sb("nsq", [P, T])
        nsr = sb("nsr", [P, T])
        nst = sb("nst", [P, T])
        snsq = sb("snsq", [P, T])
        sqp = sb("sqp", [P, T, P], BF16)
        sqT = sb("sqT", [P, S], BF16)
        rm = sb("rm", [P, T])
        rma = sb("rma", [P, T])
        rmb = sb("rmb", [P, T])
        diag = sb("diag", [P, T, P])
        ab = sb("ab", [P, S])
        w = sb("w", [P, T, S])
        oT = sb("oT", [P, S])
        dn = sb("dn", [P, S])
        rd1 = sb("rd1", [P, T])
        x1 = sb("x1", [P, T, D])
        st2 = sb("st2", [P, T, 6])
        mv2 = sb("mv2", [P, T, 2])
        ve2 = sb("ve2", [P, T])
        rs2 = sb("rs2", [P, T])
        y2 = sb("y2", [P, T, D])
        y2T = sb("y2T", [P, S])
        qf = sb("qf", [P, S])
        qr = sb("qr", [P, S])
        qpart = sb("qpart", [P, 3, S], BF16)
        nm = sb("nm", [P, T, H])
        nmr = sb("nmr", [P, T, H])
        mcat = sb("mcat", [P, T, 3, H], BF16)
        mT = sb("mT", [3 * H, S], BF16)
        qs = sb("qs", [P, 2, PAIRS, S], BF16)
        x1b = sb("x1b", [P, 2, T, D])
        PT_RING = 2 * (G + 1)
        pt = sb("pt", [P, PT_RING, S])
        pvs = sb("pvs", [P, 2, S])
        rd2 = sb("rd2", [P, T, PAIRS])
        ao = sb("ao", [P, T, P])
        aoT = sb("aoT", [P, S])
        x2 = sb("x2", [P, 2, T, D])
        st3 = sb("st3", [P, T, 6])
        mv3 = sb("mv3", [P, T, 2])
        ve3 = sb("ve3", [P, T])
        rs3 = sb("rs3", [P, T])
        y3 = sb("y3", [P, T, D])
        y3T = sb("y3T", [P, S])
        lg = sb("lg", [P, T, E])
        cmp_eq = sb("cmp_eq", [P, T, E, E])
        cmp_gt = sb("cmp_gt", [P, T, E, E])
        rank = sb("rank", [P, T, E])
        maskp = sb("maskp", [P, T, P], BF16)
        maskT16 = sb("maskT16", [P, S], BF16)
        mask_all = sb("mask_all", [P, E, S], BF16)
        ym = sb("ym", [P, E, S])
        fT = sb("fT", [P, S])
        ob = sb("ob", [P, 2, T, D])

        k_scratch = nc.dram_tensor("k_scratch", [B, P, COPY, JP], BF16, kind="Internal").ap()
        q_scratch = nc.dram_tensor("q_scratch", [P, COPY, S], BF16, kind="Internal").ap()
        m_scratch = nc.dram_tensor("m_scratch", [3 * 2, PAIRS * S], BF16, kind="Internal").ap()
        e_scratch = nc.dram_tensor("e_scratch", [E, S], BF16, kind="Internal").ap()

        x_in = [sem(f"x_in{b}") for b in range(B)]
        gamma_in, weights_in, ctx_in = sem("gamma_in"), sem("weights_in"), sem("ctx_in")
        kaug_in, qaug_in = sem("kaug_in"), sem("qaug_in")
        k_out, q_out, m_out, e_out = sem("k_out"), sem("q_out"), sem("m_out"), sem("e_out")
        e_in = [sem(f"e_in{i}") for i in range(2)]
        bias_ready, diag_done = sem("bias_ready"), sem("diag_done")
        zeroed, consts = sem("zeroed"), sem("consts")
        gamma_ready, bqs_ready = sem("gamma_ready"), sem("bqs_ready")
        setup_ps, setup_sb = sem("setup_ps"), sem("setup_sb")
        k_ready, v_ready = sem("k_ready"), sem("v_ready")
        kA_in, kB_in, qs_in, m_in = sem("kA_in"), sem("kB_in"), sem("qs_in"), sem("m_in")
        stored = [sem(f"stored{i}") for i in range(2)]
        stats = [sem(f"stats{i}") for i in range(3)]
        rstd = [sem(f"rstd{i}") for i in range(3)]
        normed = [sem(f"normed{i}") for i in range(3)]
        y1T_ps, sqT_ps, y1T_sb, sq_ready = sem("y1T_ps"), sem("sqT_ps"), sem("y1T_sb"), sem("sq_ready")
        dist_ps, rm_ready, w_relu, rowmax = sem("dist_ps"), sem("rm_ready"), sem("w_relu"), sem("rowmax")
        diag_ready, ab_ps, ab_sb = sem("diag_ready"), sem("ab_ps"), sem("ab_sb")
        w_sub_v, w_sub_p, p_ready, self_ps, oT_sb, dn_sb = (
            sem("w_sub_v"), sem("w_sub_p"), sem("p_ready"), sem("self_ps"), sem("oT_sb"), sem("dn_sb"))
        gather_ps, x1_ready, x1b_ready = sem("gather_ps"), sem("x1_ready"), sem("x1b_ready")
        y2T_ps, y2T_sb, q_ps, qf_ready = sem("y2T_ps"), sem("y2T_sb"), sem("q_ps"), sem("qf_ready")
        q_hi, q_rest, q_mid, q_lo = sem("q_hi"), sem("q_rest"), sem("q_mid"), sem("q_lo")
        a_ps, maxed, mcat_ready, mT_ps, mT_sb = sem("a_ps"), sem("maxed"), sem("mcat_ready"), sem("mT_ps"), sem("mT_sb")
        st_ps, exps, pv_ps, pvs_sb = sem("st_ps"), sem("exps"), sem("pv_ps"), sem("pvs_sb")
        nd_ps, ao_ready, ao_ps, aoT_sb, wo_ps, x2_ready = (
            sem("nd_ps"), sem("ao_ready"), sem("ao_ps"), sem("aoT_sb"), sem("wo_ps"), sem("x2_ready"))
        y3T_ps, y3T_sb, lg_ps, mask_ready, mask_ps, mask_sb = (
            sem("y3T_ps"), sem("y3T_sb"), sem("lg_ps"), sem("mask_ready"), sem("mask_ps"), sem("mask_sb"))
        masked_v, masked_p, f_ps, fT_sb, fT_ps, out_ready = (
            sem("masked_v"), sem("masked_p"), sem("f_ps"), sem("fT_sb"), sem("fT_ps"), sem("out_ready"))
        act_own, dve_own, pool_own = sem("act_own"), sem("dve_own"), sem("pool_own")

        def own(engine, semaphore):
            n = [0]

            def done(ins):
                n[0] += 1
                ins.then_inc(semaphore, 1)

            def settle():
                engine.wait_ge(semaphore, n[0])
            return done, settle

        def tile(t):
            return slice(t * P, (t + 1) * P)

        def col16(tensor):
            return tensor[:, :].bitcast(BF16)

        GROUP = S // J
        GROUPS = -(-T * H // GROUP)
        MAX_GROUPS = [range(g, min(g + 2, GROUPS)) for g in range(0, GROUPS, 2)]
        ITEMS = G + 1
        PARTS = ((0, 1), (2, 3), (4,))
        RUNS = ((0, 3), (3, 2), (5, 1))
        ONE = 16
        W_LOADS = 13
        block = stack.enter_context(nc.Block())

        @block.sync
        def _(sp):
            def load(dst, src, s):
                sp.dma_start(dst, src).then_inc(s, ONE)

            load(xs[:, 0], x[0].rearrange("(t p) d -> p t d", p=P), x_in[0])
            load(gam[:, :], gamma.partition_broadcast(P), gamma_in)
            for i, m in enumerate((Wq, Wk, Wv)):
                load(wraw[:, i, :], m, weights_in)
            wo_view = Wo.rearrange("o (g f c) -> o f g c", g=G, f=2)
            for f in range(2):
                load(wraw[:, 3, f * HALF:(f + 1) * HALF].rearrange("o (g c) -> o g c", g=G), wo_view[:, f], weights_in)
            load(bqc[:, :], bq.rearrange("(p a) -> p a", a=1), weights_in)
            load(bkc[:, :], bk.rearrange("(p a) -> p a", a=1), weights_in)
            load(bvb[:, :], bv.partition_broadcast(P), weights_in)
            load(bob[:, :], bo.partition_broadcast(P), weights_in)
            load(rbb[:, :], rb.partition_broadcast(P), weights_in)
            load(ewraw[:, :, :], ew.rearrange("e h d -> h e d"), weights_in)
            load(partsel[:, :], part_rows, weights_in)
            load(ctx_m[:, :, :], ctx[:, 0:JM, :].rearrange("b j d -> j b d"), ctx_in)
            sp.wait_ge(zeroed, 2)
            load(ctx_t[0:JT, :, :], ctx[:, JM:J, :].rearrange("b j d -> j b d"), ctx_in)
            load(rwraw[0:E, :], rw, weights_in)
            for i in range(3):
                load(ebraw[i * E:(i + 1) * E, :], eb, ctx_in)
            load(kA[:, :, :, :], k_aug[0], kaug_in)
            load(kB[:, :, :, :], k_aug[1], kaug_in)
            for par in range(2):
                load(qs[AUG:P, par, :, :], q_aug, qaug_in)
            for b in range(1, B):
                load(xs[:, b], x[b].rearrange("(t p) d -> p t d", p=P), x_in[b])

            def write_keys(b):
                for r, n in RUNS:
                    load(k_scratch[b][:, r:r + n, :], kpart[:, 0:n, b, :], k_out)

            def stack_keys(stacks, b, s_in):
                for s in range(2):
                    load(stacks[s * ROWS:(s + 1) * ROWS, s, :, :],
                         k_scratch[b].rearrange("(a s c) k j -> s (c k) a j", s=2, c=DK)[s], s_in)

            def stats1(b, _):
                if b >= 1:
                    sp.wait_ge(k_out, 3 * B * ONE)
                    sp.wait_ge(maxed, b * GROUPS)
                    stack_keys(kA, b, kA_in)

            def keys(b, _):
                sp.wait_ge(k_ready, 1)
                write_keys(0)
                sp.wait_ge(k_out, 3 * ONE)
                sp.wait_ge(kaug_in, 2 * ONE)
                stack_keys(kA, 0, kA_in)
                stack_keys(kB, 0, kB_in)

            def more_keys(b, _):
                for b in range(1, B):
                    write_keys(b)

            def query(b, _):
                for part, (got, (r, n)) in enumerate(zip((q_hi, q_mid, q_lo), RUNS)):
                    sp.wait_ge(got, b + 1)
                    load(q_scratch[:, r:r + n, :], qpart[:, part, :].unsqueeze(1).broadcast_to([P, n, S]), q_out)
                if b == 0:
                    sp.wait_ge(qaug_in, 2 * ONE)
                if b >= 2:
                    sp.wait_ge(st_ps, (b - 1) * R * ITEMS)
                sp.wait_ge(q_out, 3 * ONE * (b + 1))
                for s in range(2):
                    load(qs[s * ROWS:(s + 1) * ROWS, b % 2, :, :],
                         q_scratch.rearrange("(a s c) k n -> s (c k) a n", s=2, c=DK)[s], qs_in)

            def divide(b, f):
                if f == 0 and b + 1 < B:
                    sp.wait_ge(st_ps, (b + 1) * R * ITEMS)
                    stack_keys(kB, b + 1, kB_in)

            def mT_(b, _):
                sp.wait_ge(mT_sb, b + 1)
                load(m_scratch.rearrange("r (a n) -> (r a) n", n=S), mT[:, :], m_out)
                sp.wait_ge(m_out, ONE * (b + 1))
                load(qs[MAXROW:MAXROW + 6, b % 2, :, :].rearrange("p a n -> p (a n)"), m_scratch, m_in)

            def mask(b, _):
                sp.wait_ge(mask_sb, b + 1)
                load(e_scratch, maskT16[0:E, :], e_out)
                if b >= 1:
                    sp.wait_ge(masked_v, b * E // 2)
                    sp.wait_ge(masked_p, b * E // 2)
                sp.wait_ge(e_out, ONE * (b + 1))
                for i in range(2):
                    half = slice(i * E // 2, (i + 1) * E // 2)
                    load(mask_all[:, half, :], e_scratch[half, :].partition_broadcast(P), e_in[i])

            def store(b, _):
                sp.wait_ge(out_ready, b + 1)
                load(out[b].rearrange("(t p) d -> p t d", p=P), ob[:, b % 2], stored[b % 2])

            walk("sync", {"stats1": stats1, "keys": keys, "more_keys": more_keys, "query": query, "divide": divide, "mT": mT_, "mask": mask,
                  "store": store})
            for s in stored:
                sp.wait_ge(s, ONE * B // 2)

        @block.gpsimd
        def _(pool):
            done, settle = own(pool, pool_own)
            g = nc.gpsimd
            done(g.memset(ident[:, :], 0.0))
            done(g.memset(ident16[:, :], 0.0))
            g.memset(ctx_t[:, :, :], 0.0).then_inc(zeroed, 1)
            g.memset(rwraw[:, :], 0.0).then_inc(zeroed, 1)
            done(g.memset(minus_half[:, :], -0.5))
            settle()
            for m in (ident, ident16):
                g.affine_select(out=m[:, :], in_=m[:, :], compare_op=ALU.not_equal, fill=1.0, base=0,
                                pattern=[[-1, P]], channel_multiplier=1).then_inc(consts, 1)
            g.memset(sqp[:, :, :], 0.0).then_inc(consts, 1)
            g.memset(ones16[:, :], 1.0).then_inc(consts, 1)
            g.memset(ones[:, :], 1.0).then_inc(consts, 1)
            g.memset(thirty_second[:, :], 1.0 / 32).then_inc(consts, 1)
            pool.wait_ge(consts, 6)
            pool.wait_ge(gamma_in, ONE)
            done(g.tensor_scalar(gam2[:, :], gam[:, :], 2.0, 1.0, ALU.mult, ALU.mult))
            done(g.tensor_scalar(gneg[:, :], gam[:, :], -float(D), 1.0, ALU.mult, ALU.mult))
            done(g.tensor_scalar(rd1[:, 0:1], gam[:, :], 0.0, None, ALU.is_lt))
            settle()
            g.tensor_scalar(sgn[:, :], rd1[:, 0:1], 2.0, -1.0, ALU.mult, ALU.add).then_inc(gamma_ready, 1)
            pool.wait_ge(gamma_ready, 1)

            def norm(i, b, mv, ve, rs):
                pool.wait_ge(stats[i], b + 1)
                done(g.tensor_scalar(ve[:, :], mv[:, :, 1], EPS, 1.0, ALU.add, ALU.mult))
                settle()
                g.tensor_tensor(rs[:, :], ve[:, :], minus_half[:, :], ALU.pow).then_inc(rstd[i], 1)

            def rstd1(b, _):
                norm(0, b, mv1, ve1, rs1)
                pool.wait_ge(rstd[0], b + 1)
                if b >= 1:
                    pool.wait_ge(rowmax, b)
                    pool.wait_ge(w_relu, T * b)
                    pool.wait_ge(sqT_ps, b)
                done(g.tensor_tensor(nsr[:, :], rs1[:, :], rs1[:, :], ALU.mult))
                settle()
                done(g.tensor_tensor(nst[:, :], nsr[:, :], mv1[:, :, 1], ALU.mult))
                settle()
                done(g.tensor_scalar(nsq[:, :], nst[:, :], gneg[:, :], 1.0, ALU.mult, ALU.mult))
                settle()
                done(g.tensor_scalar(snsq[:, :], nsq[:, :], sgn[:, :], 1.0, ALU.mult, ALU.mult))
                done(g.tensor_copy(sqp[:, :, 0], nsq[:, :]))
                settle()
                done(g.tensor_tensor(nsr[:, :], nsq[:, :], sqp[:, :, 0], ALU.subtract))
                settle()
                done(g.tensor_copy(sqp[:, :, 1], nsr[:, :]))
                settle()
                done(g.tensor_tensor(nst[:, :], nsr[:, :], sqp[:, :, 1], ALU.subtract))
                settle()
                g.tensor_copy(sqp[:, :, 2], nst[:, :]).then_inc(sq_ready, 1)

            def weights(b, _):
                pool.wait_ge(weights_in, W_LOADS * ONE)
                pool.wait_ge(ctx_in, 5 * ONE)
                g.tensor_scalar(bqs[:, :], bqc[:, :], QSCALE, 1.0, ALU.mult, ALU.mult).then_inc(bqs_ready, 1)
                done(g.memset(earlier[:, :, :], 1.0))
                done(g.memset(maskp[:, :, :], 0.0))
                done(g.memset(ebias[:, :], 0.0))
                settle()
                g.affine_select(out=earlier[:, :, :], in_=earlier[:, :, :], compare_op=ALU.is_gt, fill=0.0, base=0,
                                pattern=[[1, E], [-1, E]], channel_multiplier=0).then_inc(consts, 1)
                done(g.tensor_copy(ebpart[:, 0, :], ebraw[:, :]))
                settle()
                done(g.tensor_tensor(ebr[:, 0, :], ebraw[:, :], ebpart[:, 0, :], ALU.subtract))
                settle()
                done(g.tensor_copy(ebpart[:, 1, :], ebr[:, 0, :]))
                settle()
                done(g.tensor_tensor(ebr[:, 1, :], ebr[:, 0, :], ebpart[:, 1, :], ALU.subtract))
                settle()
                done(g.tensor_copy(ebpart[:, 2, :], ebr[:, 1, :]))
                settle()
                for i in range(3):
                    done(g.tensor_scalar(ebpart[:, i, :], ebpart[:, i, :], partsel[:, i:i + 1], 1.0, ALU.mult, ALU.mult))
                settle()
                done(g.tensor_tensor(ebsum[:, 0, :], ebpart[:, 0, :], ebpart[:, 1, :], ALU.add))
                settle()
                g.tensor_tensor(ebias[0:COPIES, :], ebsum[:, 0, :], ebpart[:, 2, :], ALU.add).then_inc(bias_ready, 1)

            def sub(b, _):
                pool.wait_ge(ab_sb, b + 1)
                pool.wait_ge(w_relu, T * (b + 1))
                for t in range(0, T, 2):
                    g.tensor_tensor(w[:, t, :], w[:, t, :], ab[:, :], ALU.subtract).then_inc(w_sub_p, 1)

            def rstd2(b, _):
                norm(1, b, mv2, ve2, rs2)
                if b == 0:
                    pool.wait_ge(weights_in, W_LOADS * ONE)
                if b >= 2:
                    pool.wait_ge(x2_ready, b - 1)
                pool.wait_ge(x1_ready, b + 1)
                g.tensor_tensor(x1b[:, b % 2], x1[:, :, :], bob[:, :].unsqueeze(1).broadcast_to([P, T, D]),
                                ALU.add).then_inc(x1b_ready, 1)

            def rstd3(b, _):
                norm(2, b, mv3, ve3, rs3)

            def select(b, _):
                pool.wait_ge(y3T_sb, b + 1)
                if b >= 1:
                    pool.wait_ge(f_ps, b)
                for e in range(1, E, 2):
                    pool.wait_ge(e_in[e // (E // 2)], ONE * (b + 1))
                    g.tensor_tensor(ym[:, e, :], mask_all[:, e, :], y3T[:, :], ALU.mult).then_inc(masked_p, 1)

            walk("gpsimd", {"rstd1": rstd1, "weights": weights, "sub": sub, "rstd2": rstd2, "rstd3": rstd3, "select": select})

        @block.scalar
        def _(act):
            act.wait_ge(consts, 6)
            nc.scalar.activation(warm[:, :], thirty_second[:, :], ACT.Exp)

            copy = lambda dst, src: nc.scalar.activation(dst, src, ACT.Copy)

            def y1T_(b, _):
                if b == 0:
                    act.wait_ge(gamma_ready, 1)
                act.wait_ge(y1T_ps, b + 1)
                copy(y1T[:, :], A0[:, :]).then_inc(y1T_sb, 1)
                nc.scalar.activation(y1Tg[:, :], A0[:, :], ACT.Copy, scale=gam2[:, :]).then_inc(y1T_sb, 1)
                act.wait_ge(sqT_ps, b + 1)
                copy(sqT[:, :], col16(A1)[:, 0:S]).then_inc(y1T_sb, 1)

            def dist(b, _):
                for t in range(T):
                    act.wait_ge(rm_ready, T * b + t + 1)
                    nc.scalar.activation(w[:, t, :], (A0, A1)[t % 2][:, :], ACT.Relu, bias=snsq[:, t:t + 1],
                                         scale=sgn[:, :]).then_inc(w_relu, 1)

            def ab_(b, _):
                act.wait_ge(ab_ps, b + 1)
                copy(ab[:, :], A0[:, :]).then_inc(ab_sb, 1)

            def sub(b, _):
                for i, t in enumerate((1, 0, 3, 2)):
                    act.wait_ge(w_sub_p if t % 2 == 0 else w_sub_v, 2 * b + i // 2 + 1)
                    nc.scalar.activation(w[:, t, :], w[:, t, :], ACT.Exp, scale=sgn[:, :]).then_inc(p_ready, 1)

            def self_(b, _):
                act.wait_ge(self_ps, b + 1)
                copy(oT[:, :], A0[:, :]).then_inc(oT_sb, 1)

            def weights(b, _):
                act.wait_ge(setup_ps, 1)
                copy(wT[:, :, :], ST[0][:, :].rearrange("p (i n) -> p i n", i=4)).then_inc(setup_sb, 1)
                for i in range(2):
                    copy(ewT[:, 4 * i:4 * i + 4, :], (ST[1], MX[0])[i][:, :].rearrange("p (i n) -> p i n", i=4)).then_inc(setup_sb, 1)
                copy(rwT[:, :], YV[:, 0:E]).then_inc(setup_sb, 1)
                copy(ctxT[:, :, 0:JM], YM[:, :].rearrange("p (b j) -> p b j", b=B)).then_inc(setup_sb, 1)
                copy(ctxT[:, :, JM:JP], MX[1][:, 0:32 * B].rearrange("p (b j) -> p b j", b=B)).then_inc(setup_sb, 1)

            def keys(b, _):
                act.wait_ge(setup_ps, 2)
                act.wait_ge(weights_in, W_LOADS * ONE)
                for i in range(2):
                    nc.scalar.activation(kf[:, 2 * i:2 * i + 2, :],
                                         (ST[1], MX[0])[i][:, 0:2 * J].rearrange("p (b j) -> p b j", b=2),
                                         ACT.Identity, bias=bkc[:, :]).then_inc(setup_sb, 1)

            def y2T_(b, _):
                act.wait_ge(y2T_ps, b + 1)
                copy(y2T[:, :], A1[:, :]).then_inc(y2T_sb, 1)

            def query(b, _):
                act.wait_ge(q_ps, b + 1)
                if b == 0:
                    act.wait_ge(bqs_ready, 1)
                if b >= 1:
                    act.wait_ge(q_out, 3 * ONE * b)
                    act.wait_ge(q_lo, b)
                nc.scalar.activation(qf[:, :], A0[:, :], ACT.Identity, bias=bqs[:, :],
                                     scale=QSCALE).then_inc(qf_ready, 1)
                act.wait_ge(qf_ready, b + 1)
                copy(qpart[:, 0, :], qf[:, :]).then_inc(q_hi, 1)

            def mT_(b, _):
                act.wait_ge(mT_ps, b + 1)
                if b >= 1:
                    act.wait_ge(m_out, ONE * b)
                copy(mT[:, :], col16(MX[0])[0:3 * H, 0:S]).then_inc(mT_sb, 1)

            def scores(b, part):
                k = part // len(PARTS)
                for i in PARTS[part % len(PARTS)]:
                    n = (b * R + k) * ITEMS + i
                    act.wait_ge(st_ps, n + 1)
                    if n >= PT_RING:
                        act.wait_ge(pv_ps, b * R + k - 1)
                    nc.scalar.activation(pt[:, n % PT_RING, :], ST[n % 2][:, :], ACT.Exp).then_inc(exps, 1)

            def values(b, k):
                if k % 2:
                    act.wait_ge(pv_ps, b * R + k + 1)
                    if b >= 1:
                        act.wait_ge(nd_ps, 2 * b)
                    copy(pvs[:, k // 2, :], YV[:, :]).then_inc(pvs_sb, 1)

            def aoT_(b, _):
                act.wait_ge(ao_ps, b + 1)
                copy(aoT[:, :], YM[:, :]).then_inc(aoT_sb, 1)

            def y3T_(b, _):
                act.wait_ge(y3T_ps, b + 1)
                if b >= 1:
                    act.wait_ge(masked_v, b * E // 2)
                    act.wait_ge(masked_p, b * E // 2)
                copy(y3T[:, :], YM[:, :]).then_inc(y3T_sb, 1)

            def mask(b, _):
                act.wait_ge(mask_ps, b + 1)
                if b >= 1:
                    act.wait_ge(e_out, ONE * b)
                    act.wait_ge(f_ps, b)
                copy(maskT16[:, :], col16(YM)[:, 0:S]).then_inc(mask_sb, 1)

            def fT_(b, _):
                act.wait_ge(f_ps, b + 1)
                copy(fT[:, :], YV[:, :]).then_inc(fT_sb, 1)

            walk("scalar", {"y1T": y1T_, "dist": dist, "ab": ab_, "sub": sub, "self": self_, "weights": weights, "keys": keys,
                  "y2T": y2T_, "query": query, "mT": mT_, "scores": scores, "values": values, "aoT": aoT_,
                  "y3T": y3T_, "mask": mask, "fT": fT_})

        @block.vector
        def _(dve):
            done, settle = own(dve, dve_own)
            v = nc.vector

            def stats_of(i, src, st, mv):
                for t in range(T):
                    done(v.bn_stats(st[:, t, :], src(t)))
                settle()
                for t in range(T):
                    last = v.bn_aggr(mv[:, t, :], st[:, t, :])
                last.then_inc(stats[i], 1)

            def normalise(i, b, src, mv, rs, y):
                dve.wait_ge(stats[i], b + 1)
                dve.wait_ge(rstd[i], b + 1)
                for t in range(T):
                    last = v.tensor_scalar(y[:, t, :], src(t), mv[:, t, 0:1], rs[:, t:t + 1], ALU.subtract, ALU.mult)
                last.then_inc(normed[i], 1)

            def stats1(b, _):
                dve.wait_ge(x_in[b], ONE)
                if b >= 1:
                    dve.wait_ge(sq_ready, b)
                stats_of(0, lambda t: xs[:, b, t, :], st1, mv1)

            def y1_(b, _):
                if b >= 1:
                    dve.wait_ge(self_ps, b)
                normalise(0, b, lambda t: xs[:, b, t, :], mv1, rs1, y1)

            def dist(b, _):
                for t in range(T):
                    dve.wait_ge(dist_ps, T * b + t + 1)
                    v.tensor_reduce(rm[:, t:t + 1], (A0, A1)[t % 2][:, :], AX.X, ALU.max).then_inc(rm_ready, 1)

            def rowmax_(b, _):
                dve.wait_ge(rm_ready, T * (b + 1))
                dve.wait_ge(sq_ready, b + 1)
                done(v.scalar_tensor_tensor(out=rma[:, :], in0=rm[:, :], scalar=sgn[:, :], in1=snsq[:, :],
                                            op0=ALU.mult, op1=ALU.add))
                settle()
                v.tensor_scalar(rmb[:, :], rma[:, :], 0.0, None, ALU.max).then_inc(rowmax, 1)
                dve.wait_ge(rowmax, b + 1)
                for t in range(T):
                    last = v.tensor_scalar(diag[:, t, :], ident[:, :], rmb[:, t:t + 1], None, ALU.mult)
                last.then_inc(diag_ready, 1)

            def sub(b, _):
                dve.wait_ge(ab_sb, b + 1)
                dve.wait_ge(w_relu, T * (b + 1))
                for t in range(1, T, 2):
                    v.tensor_tensor(w[:, t, :], w[:, t, :], ab[:, :], ALU.subtract).then_inc(w_sub_v, 1)

            def self_(b, _):
                dve.wait_ge(self_ps, b + 1)
                v.tensor_copy(dn[:, :], A1[:, :]).then_inc(dn_sb, 1)

            def gather(b, _):
                dve.wait_ge(gather_ps, b + 1)
                done(v.reciprocal(rd1[:, :], A0[:, 0:T]))
                settle()
                if b >= 1:
                    dve.wait_ge(x1b_ready, b)
                for t in range(T):
                    last = v.scalar_tensor_tensor(out=x1[:, t, :], in0=A1[:, tile(t)], scalar=rd1[:, t:t + 1],
                                                  in1=xs[:, b, t, :], op0=ALU.mult, op1=ALU.add)
                last.then_inc(x1_ready, 1)
                dve.wait_ge(x1_ready, b + 1)
                stats_of(1, lambda t: x1[:, t, :], st2, mv2)

            def y2_(b, _):
                normalise(1, b, lambda t: x1[:, t, :], mv2, rs2, y2)

            def weights(b, _):
                done(v.memset(vm[:, :, :, :], 0.0))
                done(v.memset(vt[:, :, :, :], 0.0))
                done(v.memset(kpart[:, :, :, :], 0.0))
                settle()
                for s in range(2):
                    done(v.memset(vm[:, :, s::2, 16 * s + DK:16 * s + 2 * DK], 1.0))
                    for g in range(G):
                        c = 32 * g + 16 * s
                        done(v.memset(vt[32 * g:32 * g + JT, :, s::2, c + DK:c + 2 * DK], 1.0))

            def keys(b, _):
                dve.wait_ge(setup_sb, 8)
                dve.wait_ge(weights_in, W_LOADS * ONE)
                done(v.tensor_copy(kpart[:, 0, :, 0:J], kf[:, :, :]))
                settle()
                done(v.tensor_tensor(kr[:, :, :], kf[:, :, :], kpart[:, 0, :, 0:J], ALU.subtract))
                settle()
                done(v.tensor_copy(kpart[:, 1, :, 0:J], kr[:, :, :]))
                settle()
                v.tensor_tensor(kpart[:, 2, :, 0:J], kr[:, :, :], kpart[:, 1, :, 0:J], ALU.subtract).then_inc(k_ready, 1)
                for b in range(B):
                    val = YM[:, tile(b)].rearrange("p (a s d) -> p s a d", s=2, d=DK)
                    bias = bvb[:, :].rearrange("p (a s d) -> p s a d", s=2, d=DK)
                    for s in range(2):
                        v.tensor_tensor(vm[:, b, s::2, 16 * s:16 * s + DK], val[:, s], bias[:, s],
                                        ALU.add).then_inc(v_ready, 1)
                for g in range(G):
                    rows = slice(32 * g, 32 * g + JT)
                    val = YV[rows, 0:32 * B].rearrange("p (b a s d) -> p s b a d", b=B, s=2, d=DK)
                    bias = bvb[rows, 32 * g:32 * g + 32].rearrange("p (a s d) -> p s a d", s=2, d=DK)
                    for s in range(2):
                        c = 32 * g + 16 * s
                        v.tensor_tensor(vt[rows, :, s::2, c:c + DK], val[:, s],
                                        bias[:, s].unsqueeze(1).broadcast_to([JT, B, 2, DK]),
                                        ALU.add).then_inc(v_ready, 1)

            def query(b, _):
                dve.wait_ge(q_hi, b + 1)
                v.tensor_tensor(qr[:, :], qf[:, :], qpart[:, 0, :], ALU.subtract).then_inc(q_rest, 1)
                dve.wait_ge(q_rest, b + 1)
                v.tensor_copy(qpart[:, 1, :], qr[:, :]).then_inc(q_mid, 1)
                dve.wait_ge(q_mid, b + 1)
                v.tensor_tensor(qpart[:, 2, :], qr[:, :], qpart[:, 1, :], ALU.subtract).then_inc(q_lo, 1)

            def maxima(b, k):
                negated = nm[:, :, :].rearrange("p t h -> p (t h)")
                for g in MAX_GROUPS[k]:
                    n, heads = b * GROUPS + g, min(GROUP, T * H - GROUP * g)
                    dve.wait_ge(a_ps, n + 1)
                    v.tensor_reduce(negated[:, GROUP * g:GROUP * g + heads],
                                    MX[n % 2][:, 0:heads * J].rearrange("p (s j) -> p s j", s=heads),
                                    AX.X, ALU.max, negate=True).then_inc(maxed, 1)

            def mcat_(b, _):
                neg = nm[:, :, :].rearrange("p t (a s) -> p t s a", s=2)
                rest = nmr[:, :, :].rearrange("p t (s a) -> p t s a", s=2)
                part = [mcat[:, :, i, :].rearrange("p t (s a) -> p t s a", s=2) for i in range(3)]
                dve.wait_ge(maxed, (b + 1) * GROUPS)
                done(v.tensor_copy(part[0], neg))
                settle()
                done(v.tensor_tensor(rest, neg, part[0], ALU.subtract))
                settle()
                done(v.tensor_copy(part[1], rest))
                settle()
                v.tensor_tensor(part[2], rest, part[1], ALU.subtract).then_inc(mcat_ready, 1)

            def divide(b, f):
                nd = YM[:, :].rearrange("p (t c x) -> p t c x", t=T, x=2 * DK)
                dve.wait_ge(nd_ps, 2 * b + f + 1)
                done(v.reciprocal(rd2[:, :, :], nd[:, :, :, DK]))
                settle()
                v.tensor_tensor(ao[:, :, f * HALF:(f + 1) * HALF].rearrange("p t (c d) -> p t c d", d=DK),
                                nd[:, :, :, 0:DK], rd2[:, :, :].unsqueeze(3).broadcast_to([P, T, PAIRS, DK]),
                                ALU.mult).then_inc(ao_ready, 1)

            def wo(b, _):
                dve.wait_ge(wo_ps, b + 1)
                dve.wait_ge(x1b_ready, b + 1)
                v.tensor_tensor(x2[:, b % 2], YV[:, :].rearrange("p (t d) -> p t d", t=T), x1b[:, b % 2],
                                ALU.add).then_inc(x2_ready, 1)
                dve.wait_ge(x2_ready, b + 1)
                stats_of(2, lambda t: x2[:, b % 2, t, :], st3, mv3)

            def y3_(b, _):
                normalise(2, b, lambda t: x2[:, b % 2, t, :], mv3, rs3, y3)

            def route(b, _):
                dve.wait_ge(lg_ps, b + 1)
                if b == 0:
                    dve.wait_ge(consts, 7)
                    dve.wait_ge(weights_in, W_LOADS * ONE)
                done(v.tensor_tensor(lg[:, :, :], YV[:, 0:T * E].rearrange("p (t e) -> p t e", t=T),
                                     rbb[:, :].unsqueeze(1).broadcast_to([P, T, E]), ALU.add))
                settle()
                other = lg[:, :, :].unsqueeze(2).broadcast_to([P, T, E, E])
                mine = lg[:, :, :].unsqueeze(3).broadcast_to([P, T, E, E])
                done(v.tensor_tensor(cmp_eq[:, :, :, :], other, mine, ALU.is_equal))
                done(v.tensor_tensor(cmp_gt[:, :, :, :], other, mine, ALU.is_gt))
                settle()
                done(v.tensor_tensor(cmp_eq[:, :, :, :], cmp_eq[:, :, :, :],
                                     earlier[:, :, :].unsqueeze(1).broadcast_to([P, T, E, E]), ALU.mult))
                settle()
                done(v.tensor_tensor(cmp_gt[:, :, :, :], cmp_gt[:, :, :, :], cmp_eq[:, :, :, :], ALU.add))
                settle()
                done(v.tensor_reduce(rank[:, :, :], cmp_gt[:, :, :, :], AX.X, ALU.add))
                settle()
                v.tensor_scalar(maskp[:, :, 0:COPIES].rearrange("p t (i e) -> p t i e", e=E),
                                rank[:, :, :].unsqueeze(2).broadcast_to([P, T, 3, E]), 1.5, None,
                                ALU.is_lt).then_inc(mask_ready, 1)

            def select(b, _):
                dve.wait_ge(y3T_sb, b + 1)
                if b >= 1:
                    dve.wait_ge(f_ps, b)
                for e in range(0, E, 2):
                    dve.wait_ge(e_in[e // (E // 2)], ONE * (b + 1))
                    v.tensor_tensor(ym[:, e, :], mask_all[:, e, :], y3T[:, :], ALU.mult).then_inc(masked_v, 1)

            def store(b, _):
                dve.wait_ge(fT_ps, b + 1)
                if b >= 2:
                    dve.wait_ge(stored[b % 2], ONE * (b // 2))
                v.tensor_tensor(ob[:, b % 2], YM[:, :].rearrange("p (t d) -> p t d", t=T), x2[:, b % 2],
                                ALU.add).then_inc(out_ready, 1)

            walk("vector", {"stats1": stats1, "y1": y1_, "dist": dist, "rowmax": rowmax_, "sub": sub, "self": self_,
                  "gather": gather, "y2": y2_, "weights": weights, "keys": keys, "query": query, "maxima": maxima,
                  "mcat": mcat_, "divide": divide, "wo": wo, "y3": y3_, "route": route, "select": select, "store": store})

        @block.tensor
        def _(pe):
            mm = nc.tensor.matmul
            pe.wait_ge(consts, 6)

            def turn(bank_, src, id_=ident):
                for t in range(T):
                    last = nc.tensor.transpose(bank_[:, tile(t)], src(t), id_[:, :])
                return last

            def weights(b, _):
                pe.wait_ge(weights_in, W_LOADS * ONE)
                pe.wait_ge(ctx_in, 5 * ONE)
                turn(ST[0], lambda i: wraw[:, i, :])
                turn(ST[1], lambda i: ewraw[:, i, :])
                turn(MX[0], lambda i: ewraw[:, 4 + i, :])
                nc.tensor.transpose(YV[:, 0:P], rwraw[:, :], ident[:, :])
                turn(YM, lambda i: ctx_m[:, i, :])
                for i in range(B):
                    last = nc.tensor.transpose(MX[1][:, 32 * i:32 * i + 32], ctx_t[:, i, :], ident[0:32, 0:32])
                last.then_inc(setup_ps, 1)

            def keys(b, _):
                pe.wait_ge(setup_sb, 6)
                for i in range(2):
                    mm((ST[1], MX[0])[i][:, 0:2 * J], wT[:, 1, :], ctxT[:, 2 * i:2 * i + 2, 0:J], start=True, stop=True)
                for i in range(B):
                    mm(YM[:, tile(i)], ctxT[:, i, 0:JM], wT[:, 2, :], start=True, stop=True)
                for i in range(B):
                    for g in range(G):
                        last = mm(YV[32 * g:32 * g + 32, 32 * i:32 * i + 32], ctxT[:, i, JM:JP],
                                  wT[:, 2, 32 * g:32 * g + 32], start=True, stop=True)
                last.then_inc(setup_ps, 1)

            def y1T_(b, _):
                pe.wait_ge(normed[0], b + 1)
                if b >= 1:
                    pe.wait_ge(y2T_sb, b)
                    pe.wait_ge(qf_ready, b)
                turn(A0, lambda t: y1[:, t, :]).then_inc(y1T_ps, 1)
                pe.wait_ge(sq_ready, b + 1)
                turn(col16(A1), lambda t: sqp[:, t, :], ident16).then_inc(sqT_ps, 1)

            def dist(b, _):
                pe.wait_ge(y1T_sb, 3 * (b + 1))
                for t in range(T):
                    if t >= 2:
                        pe.wait_ge(w_relu, T * b + t - 1)
                    mm((A0, A1)[t % 2][:, :], y1T[:, tile(t)], y1Tg[:, :], start=True, stop=False)
                    mm((A0, A1)[t % 2][:, :], ones16[:, :], sqT[:, :], start=False, stop=True).then_inc(dist_ps, 1)

            def ab_(b, _):
                pe.wait_ge(diag_ready, b + 1)
                pe.wait_ge(w_relu, T * (b + 1))
                mm(A0[:, :], ones[:, :], diag[:, :, :], start=True, stop=True).then_inc(ab_ps, 1)

            def self_(b, _):
                for i, t in enumerate((1, 0, 3, 2)):
                    pe.wait_ge(p_ready, T * b + i + 1)
                    mm(A0[:, :], y1[:, t, :], w[:, t, :], start=(i == 0), stop=(i == T - 1))
                for t in range(T):
                    last = mm(A1[32 * t:32 * t + 32, :], ones[:, 0:32], w[:, t, :], start=True, stop=True)
                last.then_inc(self_ps, 1)

            def gather(b, _):
                pe.wait_ge(oT_sb, b + 1)
                pe.wait_ge(dn_sb, b + 1)
                turn(A1, lambda t: oT[:, tile(t)])
                for t in range(T):
                    last = mm(A0[:, t:t + 1], dn[:, tile(t)], thirty_second[:, :], start=True, stop=True)
                last.then_inc(gather_ps, 1)

            def y2T_(b, _):
                pe.wait_ge(normed[1], b + 1)
                turn(A1, lambda t: y2[:, t, :]).then_inc(y2T_ps, 1)

            def query(b, _):
                pe.wait_ge(y2T_sb, b + 1)
                if b == 0:
                    pe.wait_ge(setup_sb, 6)
                mm(A0[:, :], wT[:, 0, :], y2T[:, :], start=True, stop=True).then_inc(q_ps, 1)

            def pieces(g):
                found, n = [], GROUP * g
                while n < min(GROUP * (g + 1), T * H):
                    heads = 2 if n % 2 == 0 and n + 2 <= min(GROUP * (g + 1), T * H) else 1
                    found.append((n // H, n % H // 2, n % 2, heads))
                    n += heads
                return found

            def maxima(b, k):
                if k == 0:
                    pe.wait_ge(kA_in, 2 * ONE * (b + 1))
                    pe.wait_ge(qs_in, 2 * ONE * (b + 1))
                    if b == 0:
                        pe.wait_ge(setup_sb, 8)
                    if b >= 1:
                        pe.wait_ge(mT_sb, b)
                for g in MAX_GROUPS[k]:
                    n = b * GROUPS + g
                    if n >= 2:
                        pe.wait_ge(maxed, n - 1)
                    at = 0
                    for t, a, s, heads in pieces(g):
                        last = mm(MX[n % 2][:, at * J:(at + heads) * J], qs[:, b % 2, a, tile(t)],
                                  kA[:, s:s + heads, a, 0:J], start=True, stop=True)
                        at += heads
                    last.then_inc(a_ps, 1)

            def mT_(b, _):
                pe.wait_ge(mcat_ready, b + 1)
                turn(col16(MX[0])[0:3 * H], lambda t: mcat[:, t, :, :].rearrange("p i h -> p (i h)"),
                     ident16).then_inc(mT_ps, 1)

            def scores(b, part):
                k = part // len(PARTS)
                if part == 0:
                    pe.wait_ge(kB_in, 2 * ONE * (b + 1))
                    pe.wait_ge(m_in, ONE * (b + 1))
                for i in PARTS[part % len(PARTS)]:
                    n = (b * R + k) * ITEMS + i
                    if n >= 2:
                        pe.wait_ge(exps, n - 1)
                    if i < G:
                        h = R * i + k
                        last = mm(ST[n % 2][:, :], kB[:, h % 2, h // 2, 0:JM], qs[:, b % 2, h // 2, :],
                                  start=True, stop=True)
                    else:
                        for g in range(G):
                            h = R * g + k
                            last = mm(ST[n % 2][32 * g:32 * g + 32, :], kB[:, h % 2, h // 2, JM:JP],
                                      qs[:, b % 2, h // 2, :], start=True, stop=True)
                    last.then_inc(st_ps, 1)

            def values(b, k):
                n = (b * R + k) * ITEMS
                if k == 0 and b == 0:
                    pe.wait_ge(v_ready, 2 * B + 2 * G)
                if k == 0 and b >= 1:
                    pe.wait_ge(fT_sb, b)
                if k == 2:
                    pe.wait_ge(pvs_sb, 2 * b + 1)
                pe.wait_ge(exps, n + ITEMS)
                for g in range(G):
                    mm(YV[32 * g:32 * g + 32, :], vm[:, b, R * g + k, :], pt[:, (n + g) % PT_RING, :],
                       start=(k % 2 == 0), stop=False, skip_group_check=True)
                mm(YV[:, :], vt[:, b, k, :], pt[:, (n + G) % PT_RING, :], start=False, stop=(k % 2 == 1),
                   skip_group_check=True).then_inc(pv_ps, 1)

            def divide(b, f):
                pe.wait_ge(pvs_sb, 2 * b + f + 1)
                if f == 0 and b >= 1:
                    pe.wait_ge(out_ready, b)
                if f == 1:
                    pe.wait_ge(ao_ready, 2 * b + 1)
                turn(YM, lambda t: pvs[:, f, tile(t)]).then_inc(nd_ps, 1)

            def aoT_(b, _):
                pe.wait_ge(ao_ready, 2 * b + 2)
                turn(YM, lambda t: ao[:, t, :]).then_inc(ao_ps, 1)

            def wo(b, _):
                pe.wait_ge(aoT_sb, b + 1)
                for t in range(T):
                    last = mm(YV[:, tile(t)], aoT[:, tile(t)], wT[:, 3, :], start=True, stop=True)
                last.then_inc(wo_ps, 1)

            def y3T_(b, _):
                pe.wait_ge(normed[2], b + 1)
                turn(YM, lambda t: y3[:, t, :]).then_inc(y3T_ps, 1)

            def route(b, _):
                pe.wait_ge(y3T_sb, b + 1)
                for t in range(T):
                    last = mm(YV[:, t * E:(t + 1) * E], y3T[:, tile(t)], rwT[:, :], start=True, stop=True)
                last.then_inc(lg_ps, 1)

            def mask(b, _):
                pe.wait_ge(mask_ready, b + 1)
                turn(col16(YM), lambda t: maskp[:, t, :], ident16).then_inc(mask_ps, 1)

            def experts(b, _):
                pe.wait_ge(mask_sb, b + 1)
                if b == 0:
                    pe.wait_ge(bias_ready, 1)
                mm(YV[:, :], ebias[:, :], maskT16[:, :], start=True, stop=False)
                for e in range(E):
                    pe.wait_ge(masked_p if e % 2 else masked_v, b * E // 2 + e // 2 + 1)
                    last = mm(YV[:, :], ewT[:, e, :], ym[:, e, :], start=False, stop=(e == E - 1))
                last.then_inc(f_ps, 1)

            def fT_(b, _):
                pe.wait_ge(fT_sb, b + 1)
                turn(YM, lambda t: fT[:, tile(t)]).then_inc(fT_ps, 1)

            walk("tensor", {"y1T": y1T_, "dist": dist, "ab": ab_, "self": self_, "gather": gather, "weights": weights,
                  "keys": keys, "y2T": y2T_, "query": query, "maxima": maxima, "mT": mT_, "scores": scores,
                  "values": values, "divide": divide, "aoT": aoT_, "wo": wo, "y3T": y3T_, "route": route,
                  "mask": mask, "experts": experts, "fT": fT_})


_INS = ['x', 'ctx_1024', 'L0_attn_gamma', 'L0_xattn_Wq', 'L0_xattn_bq', 'L0_xattn_Wk', 'L0_xattn_bk', 'L0_xattn_Wv',
        'L0_xattn_bv', 'L0_xattn_Wo', 'L0_xattn_bo', 'L0_ffn_router_w', 'L0_ffn_router_b', 'L0_ffn_expert_w',
        'L0_ffn_expert_b']
_OUTS = [((B, S, D), 'float32')]


def alibi_rows():
    import numpy as np
    slopes = 2.0 ** (np.arange(H) - 8)
    q_aug = np.zeros((P - AUG, PAIRS, S), np.float32)
    i = np.arange(S)
    q_aug[0], q_aug[1], q_aug[2] = 1.0, i % 256, i - i % 256
    k_aug = np.zeros((2, P, 2, PAIRS, JP), np.float32)
    for h in range(H):
        a, s = h // 2, h % 2
        k_aug[:, AUG, s, a, 0:J] = -slopes[h] * np.arange(J)
        k_aug[:, AUG + 1:AUG + 3, s, a, 0:J] = slopes[h]
        k_aug[1, MAXROW + s:MAXROW + 6:2, s, a, 0:J] = 1.0
    part_rows = np.repeat(np.eye(3), E, axis=0).astype(np.float32)
    bf16 = np.dtype("bfloat16")
    return q_aug.astype(bf16), k_aug.astype(bf16), part_rows


def kernel(**inputs):
    import numpy as _np
    import concourse.bacc as _bacc
    from concourse import mybir as _mybir
    from concourse.bass_utils import run_bass_kernel_spmd as _run

    nc = _bacc.Bacc("TRN2", target_bir_lowering=False, num_devices=1)
    arrays, args = {}, []

    def take(name, a):
        arrays[f"in_{name}_dram"] = a
        args.append(nc.dram_tensor(f"in_{name}_dram", a.shape, _mybir.dt.from_np(a.dtype), kind="ExternalInput").ap())

    for name in _INS:
        take(name, _np.ascontiguousarray(inputs[name]))
    for name, a in zip(("q_aug", "k_aug", "part_rows"), alibi_rows()):
        take(name, a)
    for i, (shape, dtype) in enumerate(_OUTS):
        dt = _mybir.dt.from_np(_np.dtype(dtype))
        args.append(nc.dram_tensor(f"out_{i}_dram", shape, dt, kind="ExternalOutput").ap())
    program(nc, *args)
    r = _run(nc, [arrays], core_ids=[0])
    got = tuple(r.results[0][f"out_{i}_dram"] for i in range(len(_OUTS)))
    return got[0]
```
